# Optimizing a Trainium2 kernel written in Bass

```python
import numpy as np
import jax
import jax.numpy as jnp

def _softmax(x, axis=-1):
    return jax.nn.softmax(x, axis=axis)

def _gelu(x):
    return jax.nn.gelu(x, approximate=True)

def _silu(x):
    return jax.nn.silu(x)

def _sigmoid(x):
    return jax.nn.sigmoid(x)

def _layernorm(x, axis=-1, eps=1e-05):
    m = jnp.mean(x, axis=axis, keepdims=True)
    v = jnp.var(x, axis=axis, keepdims=True)
    return (x - m) / jnp.sqrt(v + eps)

def _scatter_add(tgt, idx, src, axis=0):
    return tgt.at[idx].add(src)

def _segment_sum(src, seg, n):
    return jax.ops.segment_sum(src, seg, n)
kernel_name = 'mk_xattn_ffn_d1_seqx_r8_110481'

def setup_inputs(seed: int=0):
    np.random.seed(seed)
    _w = jnp.asarray

    def _rec_inputs():
        import jax
        import jax.numpy as jnp
        _rk = jax.random.key(seed)
        x = -0.0005207 + 1.001 * jax.random.normal(jax.random.fold_in(_rk, 1), (2, 512, 128), jnp.float32)
        _lenS = 512 - jax.random.randint(jax.random.fold_in(_rk, 7), (2,), 0, max(1, 512 // 4) + 1, jnp.int32)
        _lenS2 = 77 - jax.random.randint(jax.random.fold_in(_rk, 8), (2,), 0, max(1, 77 // 4) + 1, jnp.int32)
        _ctx_1024P = jax.random.normal(jax.random.fold_in(_rk, 11), (2, 16, 128), jnp.float32)
        _ctx_1024c = jax.random.dirichlet(jax.random.fold_in(_rk, 511), 0.3 * jnp.ones((16,), jnp.float32), (2, 77))
        _ctx_1024t = jnp.einsum('bsk,bkd->bsd', _ctx_1024c, _ctx_1024P)
        _ctx_1024t = _ctx_1024t * jax.lax.rsqrt(jnp.mean(jnp.square(_ctx_1024t)) + 1e-12) * 0.953939
        ctx_1024 = 4.13588e-05 + 0.999923 * (_ctx_1024t + 0.3 * jax.random.normal(jax.random.fold_in(_rk, 611), (2, 77, 128), jnp.float32))
        return (x, ctx_1024)
    x, ctx_1024 = _rec_inputs()

    def _L0_xattn_setup():
        import jax, jax.numpy as jnp
        import numpy as np
        DIM = 128
        DIM_CTX = 128
        DIM_HEAD = 64
        HEADS = 16
        INNER = DIM_HEAD * HEADS
        EPS = 1e-05

        def _split_heads(t):
            b, n, _ = t.shape
            return t.reshape(b, n, HEADS, DIM_HEAD).transpose(0, 2, 1, 3)
        key = jax.random.key(seed)
        ks = jax.random.split(key, 6)
        b, n, m = (2, 128, 512)
        x = jax.random.normal(ks[0], (b, n, DIM), dtype=jnp.float32)
        context = jax.random.normal(ks[1], (b, m, DIM_CTX), dtype=jnp.float32)
        W_q = jax.random.normal(ks[2], (DIM, INNER), dtype=jnp.float32) * DIM ** (-0.5)
        W_kv = jax.random.normal(ks[3], (DIM_CTX, 2 * INNER), dtype=jnp.float32) * DIM_CTX ** (-0.5)
        W_out = jax.random.normal(ks[4], (INNER, DIM), dtype=jnp.float32) * INNER ** (-0.5)
        ln_gamma = jnp.ones((DIM,), dtype=jnp.float32)
        ln_beta = jnp.zeros((DIM,), dtype=jnp.float32)
        return {'x': x, 'context': context, 'W_q': W_q, 'W_kv': W_kv, 'W_out': W_out, 'ln_gamma': ln_gamma, 'ln_beta': ln_beta}
    _L0_xattn_all = _L0_xattn_setup()
    _L0_xattn_in = {k: v for k, v in _L0_xattn_all.items() if k in ('W_q', 'W_kv', 'W_out', 'ln_gamma', 'ln_beta')}
    del _L0_xattn_all

    def _L0_ffn_setup():
        import jax, jax.numpy as jnp
        import numpy as np
        D_MODEL = 128
        D_FF = 512
        NUM_EXPERTS = 8
        TOP_K = 2
        key = jax.random.key(seed)
        ks = jax.random.split(key, 9)
        s = 0.02
        x = jax.random.normal(ks[0], (2, 256, D_MODEL), dtype=jnp.float32)
        Wg = jax.random.normal(ks[1], (D_MODEL, NUM_EXPERTS), dtype=jnp.float32) * s
        bg = jnp.zeros((NUM_EXPERTS,), dtype=jnp.float32)
        W1 = jax.random.normal(ks[2], (NUM_EXPERTS, D_MODEL, D_FF), dtype=jnp.float32) * s
        b1 = jnp.zeros((NUM_EXPERTS, D_FF), dtype=jnp.float32)
        W3 = jax.random.normal(ks[3], (NUM_EXPERTS, D_MODEL, D_FF), dtype=jnp.float32) * s
        b3 = jnp.zeros((NUM_EXPERTS, D_FF), dtype=jnp.float32)
        W2 = jax.random.normal(ks[4], (NUM_EXPERTS, D_FF, D_MODEL), dtype=jnp.float32) * s
        b2 = jnp.zeros((NUM_EXPERTS, D_MODEL), dtype=jnp.float32)
        return {'x': x, 'Wg': Wg, 'bg': bg, 'W1': W1, 'b1': b1, 'W3': W3, 'b3': b3, 'W2': W2, 'b2': b2}
    _L0_ffn_all = _L0_ffn_setup()
    _L0_ffn_in = {k: v for k, v in _L0_ffn_all.items() if k in ('Wg', 'bg', 'W1', 'b1', 'W3', 'b3', 'W2', 'b2')}
    del _L0_ffn_all
    return {'x': x, 'ctx_1024': ctx_1024, 'L0_xattn_W_q': _L0_xattn_in['W_q'], 'L0_xattn_W_kv': _L0_xattn_in['W_kv'], 'L0_xattn_W_out': _L0_xattn_in['W_out'], 'L0_xattn_ln_gamma': _L0_xattn_in['ln_gamma'], 'L0_xattn_ln_beta': _L0_xattn_in['ln_beta'], 'L0_ffn_Wg': _L0_ffn_in['Wg'], 'L0_ffn_bg': _L0_ffn_in['bg'], 'L0_ffn_W1': _L0_ffn_in['W1'], 'L0_ffn_b1': _L0_ffn_in['b1'], 'L0_ffn_W3': _L0_ffn_in['W3'], 'L0_ffn_b3': _L0_ffn_in['b3'], 'L0_ffn_W2': _L0_ffn_in['W2'], 'L0_ffn_b2': _L0_ffn_in['b2']}

def reference(x, ctx_1024, L0_xattn_W_q, L0_xattn_W_kv, L0_xattn_W_out, L0_xattn_ln_gamma, L0_xattn_ln_beta, L0_ffn_Wg, L0_ffn_bg, L0_ffn_W1, L0_ffn_b1, L0_ffn_W3, L0_ffn_b3, L0_ffn_W2, L0_ffn_b2):
    import jax
    import jax.numpy as jnp

    def _L0_xattn_ref(x, context, W_q, W_kv, W_out, ln_gamma, ln_beta):
        import jax, jax.numpy as jnp
        import numpy as np
        DIM = 128
        DIM_CTX = 128
        DIM_HEAD = 64
        HEADS = 16
        INNER = DIM_HEAD * HEADS
        EPS = 1e-05

        def _split_heads(t):
            b, n, _ = t.shape
            return t.reshape(b, n, HEADS, DIM_HEAD).transpose(0, 2, 1, 3)
        scale = DIM_HEAD ** (-0.5)
        mu = jnp.mean(x, axis=-1, keepdims=True)
        var = jnp.mean(jnp.square(x - mu), axis=-1, keepdims=True)
        xn = (x - mu) * jax.lax.rsqrt(var + EPS) * ln_gamma + ln_beta
        q = _split_heads(xn @ W_q) * scale
        kv = context @ W_kv
        k, v = jnp.split(kv, 2, axis=-1)
        k = _split_heads(k)
        v = _split_heads(v)
        sim = jnp.einsum('bhid,bhjd->bhij', q, k)
        attn = jax.nn.softmax(sim, axis=-1)
        out = jnp.einsum('bhij,bhjd->bhid', attn, v)
        b_, h_, n_, d_ = out.shape
        out = out.transpose(0, 2, 1, 3).reshape(b_, n_, h_ * d_)
        return out @ W_out

    def _L0_ffn_ref(x, Wg, bg, W1, b1, W3, b3, W2, b2):
        import jax, jax.numpy as jnp
        import numpy as np
        D_MODEL = 128
        D_FF = 512
        NUM_EXPERTS = 8
        TOP_K = 2
        logits = x @ Wg + bg
        probs = jax.nn.softmax(logits, axis=-1)
        top_v, top_i = jax.lax.top_k(probs, TOP_K)
        top_v = top_v / (top_v.sum(axis=-1, keepdims=True) + 1e-06)
        onehot = jax.nn.one_hot(top_i, NUM_EXPERTS, dtype=x.dtype)
        combine = jnp.einsum('bsk,bske->bse', top_v, onehot)
        out = jnp.zeros_like(x)
        for e in range(NUM_EXPERTS):
            h = jax.nn.silu(x @ W1[e] + b1[e]) * (x @ W3[e] + b3[e])
            out = out + combine[..., e:e + 1] * (h @ W2[e] + b2[e])
        return out
    x = x + _L0_xattn_ref(_layernorm(x, axis=-1), ctx_1024, L0_xattn_W_q, L0_xattn_W_kv, L0_xattn_W_out, L0_xattn_ln_gamma, L0_xattn_ln_beta)
    x = x + _L0_ffn_ref(_layernorm(x, axis=-1), L0_ffn_Wg, L0_ffn_bg, L0_ffn_W1, L0_ffn_b1, L0_ffn_W3, L0_ffn_b3, L0_ffn_W2, L0_ffn_b2)
    return x

_drawn_inputs = setup_inputs


def setup_inputs(seed=0):
    import zlib

    import numpy as np

    out = dict(_drawn_inputs(seed))
    spreads = {'L0_xattn_ln_gamma': (1.0, 0.2),
     'L0_xattn_ln_beta': (0.0, 0.285),
     'L0_ffn_bg': (0.0, 0.1),
     'L0_ffn_b1': (0.0, 0.8),
     'L0_ffn_b3': (0.0, 0.8),
     'L0_ffn_b2': (0.0, 0.517)}
    factors = {'L0_ffn_W1': 7.125, 'L0_ffn_W3': 7.068, 'L0_ffn_W2': 6.473}
    for name, (base, spread) in spreads.items():
        noise = np.random.default_rng([zlib.crc32(name.encode()), seed]).standard_normal(out[name].shape)
        drawn = base * np.exp(spread * noise) if base else spread * noise
        out[name] = jnp.asarray(drawn.astype(out[name].dtype))
    for name, factor in factors.items():
        out[name] = (out[name] * factor).astype(out[name].dtype)
    return out
```

```python
from contextlib import ExitStack

import concourse.bass as bass
from concourse import mybir

F32 = mybir.dt.float32
F32R = mybir.dt.float32r
ALU = mybir.AluOpType
ACT = mybir.ActivationFunctionType
AX = mybir.AxisListType

P = 128
BANK = 512
EPS = 1e-5
HALF_ROOT = -0.5
E_BASE = 2.718281828459045


def build(nc, x, ctx_in, w_q, w_kv, w_out, gamma, beta, w_g, b_g, w_1, b_1, w_3, b_3, w_2, b_2, out):
    B, S, D = x.shape
    M = ctx_in.shape[1]
    INNER = w_q.shape[1]
    DH = 64
    H = INNER // DH
    PAIRS = H // 2
    E = w_1.shape[0]
    FF = w_1.shape[2]
    FC = FF // P
    T = B * S // P
    TB = S // P
    HM = H * M
    CH = -(-HM // P)
    N = B * S
    SCALE = DH ** -0.5
    assert D == P and TB * P == BANK and E == 8

    ctx = ExitStack()
    with ctx:
        def sb(name, shape, dt=F32):
            return ctx.enter_context(nc.sbuf_tensor(name, shape, dt))

        def sem(name):
            return ctx.enter_context(nc.semaphore(name))

        psum = ctx.enter_context(nc.psum_tensor("psum", [P, 8, BANK], F32))

        ident = sb("ident", [P, P])
        neg_half = sb("neg_half", [P, T])
        euler = sb("euler", [P, TB, E])
        x_sb = sb("x_sb", [P, T, P])
        ctx_sb = sb("ctx_sb", [M, B, P])
        wq_sb = sb("wq_sb", [P, INNER])
        wkv_sb = sb("wkv_sb", [P, 2 * INNER])
        wout_sb = sb("wout_sb", [P, PAIRS, P])
        wg_sb = sb("wg_sb", [P, E])
        bg_sb = sb("bg_sb", [P, E])
        VECS = 2 * E * FC + E + 2
        vec_rows = sb("vec_rows", [VECS, P])
        vecs = sb("vecs", [P, VECS])
        b13T = vecs[:, 0:2 * E * FC].rearrange("p (a n) -> p a n", a=2)
        b2T = vecs[:, 2 * E * FC:2 * E * FC + E]
        gamma_sb = vecs[:, VECS - 2:VECS - 1]
        beta_sb = vecs[:, VECS - 1:VECS]
        ctxT = sb("ctxT", [P, B * M])
        wqT = sb("wqT", [P, PAIRS, P])
        kT = sb("kT", [P, PAIRS, B * M])
        vT = sb("vT", [P, PAIRS, B * M])
        g_hi = sb("g_hi", [P, B, HM], F32R)
        g_lo = sb("g_lo", [P, B, HM], F32R)
        voT = sb("voT", [P, B, HM])
        vo = sb("vo", [P, B, CH, P])
        stats = sb("stats", [P, T, 6])
        mv = sb("mv", [P, T, 2])
        rstd = sb("rstd", [P, T])
        xn = sb("xn", [P, T, P])
        xnT = sb("xnT", [P, T, P])
        xn_hi = sb("xn_hi", [P, T, P], F32R)
        xn_lo = sb("xn_lo", [P, T, P], F32R)
        NP_ = 4
        prob = sb("prob", [P, NP_, HM])
        probT = sb("probT", [P, 2, CH, P])
        negmax = sb("negmax", [P, T, H])
        rowsum = sb("rowsum", [P, T, H])
        x2 = sb("x2", [P, T, P])
        xf = sb("xf", [P, T, P])
        xfT = sb("xfT", [P, N])
        xf_hi = sb("xf_hi", [P, N], F32R)
        xf_lo = sb("xf_lo", [P, N], F32R)
        lg = sb("lg", [P, TB, E])
        pr = sb("pr", [P, TB, E])
        red = sb("red", [P, TB])
        cmp_a = sb("cmp_a", [P, TB * E, E])
        cmp_b = sb("cmp_b", [P, TB * E, E])
        lower = sb("lower", [P, E, E])
        rank = sb("rank", [P, TB, E])
        comb = sb("comb", [P, T, E])
        logit = [lg, sb("lg1", [P, TB, E])]
        expo = [pr, sb("pr1", [P, TB, E])]
        combT = sb("combT", [E, N])
        comb_dram = nc.dram_tensor("comb_scratch", [E, N], F32, kind="Internal")
        cb = sb("cb", [P, E, N])
        b1_now = sb("b1_now", [P, FC])
        w_raw = sb("w_raw", [P, FC, 3, P])
        w_hi = sb("w_hi", [P, FC, 3, P], F32R)
        w_lo = sb("w_lo", [P, FC, 3, P], F32R)
        HB = 4
        old_prob = prob[:, :, :].rearrange("p n c -> p (n c)")
        silu, h, y_c = (old_prob[:, 2 * BANK * i:2 * BANK * (i + 1)].rearrange("p (n c) -> p n c", n=2) for i in range(3))
        h_hi, h_lo = (g[:, :, :].rearrange("p b c -> p (b c)")[:, 0:HB * BANK].rearrange("p (n c) -> p n c", n=HB)
                      for g in (g_hi, g_lo))
        acc = sb("acc", [P, 2, BANK])

        ld = {n: sem("ld_" + n) for n in ("x0", "x1", "ctx", "wq", "wk", "wv", "wout", "router", "vecs")}
        ident_ok = sem("ident_ok")
        ident_z = sem("ident_z")
        const_ok = sem("const_ok")
        pre_mm = sem("pre_mm")
        pre_act = sem("pre_act")
        pre_dve = sem("pre_dve")
        ln_stat = sem("ln_stat")
        ln_mv = sem("ln_mv")
        ln_pool = sem("ln_pool")
        ln_out = sem("ln_out")
        s_mm = sem("s_mm")
        s_dve = sem("s_dve")
        s_sub = sem("s_sub")
        s_exp = sem("s_exp")
        s_rcp = sem("s_rcp")
        s_norm = sem("s_norm")
        st_mm = sem("st_mm")
        st_free = sem("st_free")
        x2_ok = sem("x2_ok")
        xf_hi_ok = sem("xf_hi_ok")
        xf_lo_ok = sem("xf_lo_ok")
        r_act = sem("r_act")
        r_exp1 = sem("r_exp1")
        r_dve = sem("r_dve")
        r_pr = sem("r_pr")
        comb_ok = sem("comb_ok")
        comb_st = sem("comb_st")
        cb_first = sem("cb_first")
        cb_ok = sem("cb_ok")
        raw_ok = [sem(f"raw_ok{c}") for c in range(FC)]
        hi_w = sem("hi_w")
        w_split = sem("w_split")
        b1_ok = sem("b1_ok")
        g1a = sem("g1a")
        g1b = sem("g1b")
        silu_ok = sem("silu_ok")
        gate_ok = sem("gate_ok")
        hhi_ok = sem("hhi_ok")
        hlo_ok = sem("hlo_ok")
        g2_ok = sem("g2_ok")
        y_used = sem("y_used")
        acc_z = sem("acc_z")
        acc_ok = sem("acc_ok")
        o_mm = sem("o_mm")
        o_ok = sem("o_ok")
        stored = sem("stored")

        PER = BANK // (B * M)
        kv_groups = [range(i, min(i + PER, PAIRS)) for i in range(0, PAIRS, PER)]
        h_groups = [(par, g) for g in kv_groups for par in range(2)]

        def head_cols(a, b, par, g):
            return a[:, b, :].rearrange("p (k two m) -> p two k m", two=2, m=M)[:, par, g.start:g.stop, :]

        def bank_heads(bank, b, g):
            return bank[:, 0:len(g) * B * M].rearrange("p (h b m) -> p h b m", b=B, m=M)[:, :, b, :]

        plan = [("ctxT", 0)] + [("kT", i) for i in range(len(kv_groups))] + [("wqT", i) for i in range(PAIRS // 4)]
        plan += [("vecs", 0)]
        for i in range(len(h_groups)):
            plan += [("g", i)] + ([("xnT", i // 2)] if i % 2 and i // 2 < B else [])
        emptied_by = {"ctxT": "a", "vecs": "a", "wqT": "a", "kT": "a", "g": "ad", "xnT": "a"}
        PB = 8

        def empties(n, who):
            return sum(who in emptied_by[k] for k, _ in plan[:n + 1])

        place = {key: n for n, key in enumerate(plan)}
        assert len(h_groups) >= 2 * B

        ROUTE_AT = {T - 3: "xfT", T - 2: "logits"}
        FIRST_ORDER = [(0, 0), (1, 0), (2, 0), (0, 1), (1, 1), (2, 1), (3, 0), (3, 1)]
        FIRST_DONE = [1 + max(j for j, (c, _) in enumerate(FIRST_ORDER) if c == k) for k in range(FC)]
        LAG_T = 3
        ORDER = [(j // 2, j % 2) for j in range(2 * FC)]

        vo_groups = [(b, range(i, min(i + 4, CH))) for b in range(B) for i in range(0, CH, 4)]
        stage = [("vT", i) for i in range(len(kv_groups))] + [("voT", i) for i in range(len(h_groups))]
        stage += [("vo", i) for i in range(len(vo_groups))]
        pt_groups = [range(i, min(i + 4, CH)) for i in range(0, CH, 4)]
        for t in range(T):
            stage += [("pT", t, i) for i in range(len(pt_groups))] + [("y", t)]
            if t in ROUTE_AT:
                stage += [(ROUTE_AT[t], 0)]
        stage += [("xfT", 1), ("logits", 1), ("combT", 0), ("combT", 1)]
        slot = {key: n for n, key in enumerate(stage)}

        def stage_bank(key):
            return psum[:, 6 + slot[key] % 2, :]

        def rows(c):
            return min(P, HM - c * P)

        RANKED = 2 + 2 * TB

        block = ctx.enter_context(nc.Block())

        @block.sync
        def _(sp):
            x_v = x.rearrange("b (t p) d -> p (b t) d", p=P)
            sp.dma_start(x_sb[:, 0:TB, :], x_v[:, 0:TB, :]).then_inc(ld["x0"], 16)
            sp.dma_start(wkv_sb[:, 0:INNER], w_kv[:, 0:INNER]).then_inc(ld["wk"], 16)
            row = 0
            for src in (b_1.rearrange("e (c p) -> (e c) p", p=P), b_3.rearrange("e (c p) -> (e c) p", p=P), b_2[:, :],
                        gamma.rearrange("(o p) -> o p", o=1), beta.rearrange("(o p) -> o p", o=1)):
                sp.dma_start(vec_rows[row:row + src.shape[0], :], src).then_inc(ld["vecs"], 16)
                row += src.shape[0]
            sp.dma_start(wkv_sb[:, INNER:2 * INNER], w_kv[:, INNER:2 * INNER]).then_inc(ld["wv"], 16)
            sp.dma_start(wout_sb[:, :, :], w_out.rearrange("(c p) d -> p c d", p=P)).then_inc(ld["wout"], 16)
            sp.dma_start(wg_sb[:, :], w_g[:, :]).then_inc(ld["router"], 16)
            sp.dma_start(bg_sb[:, :], b_g.partition_broadcast(P)).then_inc(ld["router"], 16)

            def load_expert(e):
                for c in range(FC):
                    cols = slice(c * P, (c + 1) * P)
                    if not isinstance(e, int) or e > 0:
                        sp.wait_ge(w_split, FC * e + (c + 1 - FC))
                    sp.dma_start(w_raw[:, c, 0, :], w_1[bass.ds(e, 1), :, cols].rearrange("a k n -> (a k) n")).then_inc(raw_ok[c], 16)
                    sp.dma_start(w_raw[:, c, 1, :], w_3[bass.ds(e, 1), :, cols].rearrange("a k n -> (a k) n")).then_inc(raw_ok[c], 16)
                    sp.dma_start(w_raw[:, c, 2, :], w_2[bass.ds(e, 1), cols, :].rearrange("a k n -> (a k) n")).then_inc(raw_ok[c], 16)

            load_expert(0)
            load_expert(1)
            for b in range(B):
                half = slice(b * BANK, (b + 1) * BANK)
                sp.wait_ge(st_free, slot[("combT", b)] + 1)
                sp.dma_start(comb_dram[:, half], combT[:, half]).then_inc(comb_st, 16)
                sp.wait_ge(comb_st, 16 * (b + 1))
                for e in range(E):
                    sp.dma_start(cb[:, e, half], comb_dram[e:e + 1, half].partition_broadcast(P)).then_inc(cb_ok if e else cb_first, 16)
            with sp.Fori(2, E) as e:
                load_expert(e)
            out_v = out.rearrange("b (t p) d -> p (b t) d", p=P)
            for b in range(B):
                sp.wait_ge(o_ok, b + 1)
                sp.dma_start(out_v[:, b * TB:(b + 1) * TB, :], xn[:, b * TB:(b + 1) * TB, :]).then_inc(stored, 16)
            sp.wait_ge(stored, 16 * B)

        @block.gpsimd
        def _(pool):
            pool.memset(ident[:, :], 0.0).then_inc(ident_z, 1)
            pool.wait_ge(ident_z, 1)
            pool.affine_select(out=ident[:, :], in_=ident[:, :], compare_op=ALU.not_equal, fill=1.0,
                               base=0, pattern=[[-1, P]], channel_multiplier=1).then_inc(ident_ok, 1)
            pool.memset(neg_half[:, :], HALF_ROOT).then_inc(const_ok, 1)
            pool.memset(lower[:, :, :], 1.0).then_inc(const_ok, 1)
            pool.wait_ge(const_ok, 2)
            pool.affine_select(out=lower[:, :, :], in_=lower[:, :, :], compare_op=ALU.is_gt, fill=0.0,
                               base=0, pattern=[[1, E], [-1, E]], channel_multiplier=0).then_inc(const_ok, 1)
            pool.memset(euler[:, :, :], E_BASE).then_inc(const_ok, 1)
            pool.memset(acc[:, :, :], 0.0).then_inc(acc_z, 1)

            groups = [0]

            def rstd_step(tiles):
                n = groups[0]
                groups[0] += 1
                pool.wait_ge(ln_mv, TB * (n + 1))
                pool.tensor_scalar(rstd[:, tiles], mv[:, tiles, 1], EPS, None, ALU.add).then_inc(ln_pool, 1)
                pool.wait_ge(ln_pool, 2 * n + 1)
                pool.tensor_tensor(rstd[:, tiles], rstd[:, tiles], neg_half[:, tiles], ALU.pow).then_inc(ln_pool, 1)

            first, second = slice(0, TB), slice(TB, T)
            for tiles in (first, second, first, second):
                rstd_step(tiles)

            def lo_part(e, c):
                pool.wait_ge(hi_w, FC * e + (c + 1))
                pool.tensor_tensor(w_lo[:, c, :, :], w_raw[:, c, :, :], w_hi[:, c, :, :].bitcast(F32),
                                   ALU.subtract).then_inc(w_split, 1)

            def add_x(t):
                pool.wait_ge(st_free, slot[("y", t)] + 1)
                pool.tensor_tensor(x2[:, t, :], x_sb[:, t, :], xf[:, t, :], ALU.add).then_inc(x2_ok, 1)

            for t in range(T):
                if t >= LAG_T:
                    add_x(t - LAG_T)
                if t - LAG_T == TB - 1:
                    rstd_step(first)
                pool.wait_ge(s_rcp, t + 1)
                pool.tensor_tensor(prob[:, t % NP_, :].rearrange("p (h m) -> p h m", h=H),
                                   prob[:, t % NP_, :].rearrange("p (h m) -> p h m", h=H),
                                   rowsum[:, t, :].rearrange("p (h o) -> p h o", o=1).broadcast_to([P, H, M]),
                                   ALU.mult).then_inc(s_norm, 1)
                if LAG_T <= t < LAG_T + FC:
                    lo_part(0, t - LAG_T)
            for t in range(T - LAG_T, T):
                add_x(t)
            rstd_step(second)
            pool.wait_ge(r_pr, 2)
            pool.tensor_tensor(expo[1][:, :, :], euler[:, :, :], expo[1][:, :, :], ALU.pow).then_inc(r_exp1, 1)

            pool.wait_ge(acc_z, 1)
            pool.sem_inc(acc_ok, 2)

            def accumulate(e):
                for b in range(B):
                    pool.wait_ge(y_used, 2 * e + (b + 3))
                    pool.wait_ge(acc_ok, 2 * e + (b + 1))
                    pool.tensor_tensor(acc[:, b, :], acc[:, b, :], y_c[:, b, :], ALU.add).then_inc(acc_ok, 1)

            for c in range(FC // 2):
                lo_part(1, c)
            with pool.Fori(1, E - 1) as e:
                for c in range(FC // 2, FC):
                    lo_part(e, c)
                accumulate(e - 1)
                for c in range(FC // 2):
                    lo_part(e + 1, c)
            for c in range(FC // 2, FC):
                lo_part(E - 1, c)
            accumulate(E - 2)
            accumulate(E - 1)

        @block.scalar
        def _(act):
            act.dma_start(ctx_sb[:, :, :], ctx_in.rearrange("b m d -> m b d")).then_inc(ld["ctx"], 16)
            act.dma_start(x_sb[:, TB:T, :], x.rearrange("b (t p) d -> p (b t) d", p=P)[:, TB:T, :]).then_inc(ld["x1"], 16)
            act.dma_start(wq_sb[:, :], w_q[:, :]).then_inc(ld["wq"], 16)

            for n, (kind, i) in enumerate(plan):
                bank = psum[:, n % PB, :]
                act.wait_ge(pre_mm, n + 1)
                if kind == "ctxT":
                    ins = act.activation(ctxT[:, :], bank[:, 0:B * M], ACT.Copy)
                elif kind == "vecs":
                    ins = act.activation(vecs[:, :], bank[:, 0:VECS], ACT.Copy)
                elif kind == "wqT":
                    ins = act.activation(wqT[:, 4 * i:4 * i + 4, :], bank.rearrange("p (a d) -> p a d", d=P), ACT.Copy)
                elif kind == "kT":
                    g = kv_groups[i]
                    ins = act.activation(kT[:, g.start:g.stop, :],
                                         bank[:, 0:len(g) * B * M].rearrange("p (a m) -> p a m", a=len(g)), ACT.Copy)
                elif kind == "xnT":
                    if i == 0:
                        act.wait_ge(pre_act, place[("vecs", 0)] + 1)
                    for dst in (xn_hi, xnT):
                        ins = act.activation(dst[:, TB * i:TB * i + TB, :], bank.rearrange("p (a d) -> p a d", d=P),
                                             ACT.Identity, scale=gamma_sb, bias=beta_sb)
                else:
                    par, g = h_groups[i]
                    for b in range(B):
                        ins = act.activation(head_cols(g_hi, b, par, g), bank_heads(bank, b, g), ACT.Copy, scale=SCALE)
                ins.then_inc(pre_act, 1)

            def logits_of(b):
                return stage_bank(("logits", b))[:, 0:TB * E].rearrange("p (t e) -> p t e", e=E)

            def w_hi_part(e, c, past=None):
                act.wait_ge(raw_ok[c], 48 * e + 48)
                if past is not None:
                    act.wait_ge(g2_ok, HB + past)
                elif not isinstance(e, int) or e > 0:
                    act.wait_ge(g2_ok, HB + 2 * FC * e + (2 * c + 2 - 2 * FC))
                act.activation(w_hi[:, c, :, :], w_raw[:, c, :, :], ACT.Copy).then_inc(hi_w, 1)

            def empty_stage(key, dst, src):
                act.wait_ge(st_mm, slot[key] + 1)
                act.activation(dst, src, ACT.Copy).then_inc(st_free, 1)

            def empty_xfT(b):
                half = slice(b * BANK, (b + 1) * BANK)
                act.wait_ge(st_mm, slot[("xfT", b)] + 1)
                act.activation(xf_hi[:, half], stage_bank(("xfT", b)), ACT.Copy).then_inc(xf_hi_ok, 1)
                act.activation(xfT[:, half], stage_bank(("xfT", b)), ACT.Copy).then_inc(st_free, 1)

            def exps(t):
                act.wait_ge(s_sub, t + 1)
                act.activation(prob[:, t % NP_, :], prob[:, t % NP_, :], ACT.Exp).then_inc(s_exp, 1)

            for i, g in enumerate(kv_groups):
                empty_stage(("vT", i), vT[:, g.start:g.stop, :],
                            stage_bank(("vT", i))[:, 0:len(g) * B * M].rearrange("p (a m) -> p a m", a=len(g)))
            exps(0)
            for i, (par, g) in enumerate(h_groups):
                act.wait_ge(st_mm, slot[("voT", i)] + 1)
                for b in range(B):
                    ins = act.activation(head_cols(voT, b, par, g), bank_heads(stage_bank(("voT", i)), b, g), ACT.Copy)
                ins.then_inc(st_free, 1)
            exps(1)

            def empty_chunks(key, g, dst):
                full = [c for c in g if rows(c) == P]
                src = stage_bank(key).rearrange("p (a d) -> p a d", d=P)
                ins = act.activation(dst[:, full[0]:full[-1] + 1, :], src[:, 0:len(full), :], ACT.Copy)
                if len(full) < len(g):
                    c = g[-1]
                    ins = act.activation(dst[0:rows(c), c, :], src[0:rows(c), len(full), :], ACT.Copy)
                ins.then_inc(st_free, 1)

            for i, (b, g) in enumerate(vo_groups):
                act.wait_ge(st_mm, slot[("vo", i)] + 1)
                empty_chunks(("vo", i), g, vo[:, b])
            exps(2)
            for t in range(T):
                for i, g in enumerate(pt_groups):
                    act.wait_ge(st_mm, slot[("pT", t, i)] + 1)
                    if i == 0 and t >= 2:
                        act.wait_ge(st_mm, slot[("y", t - 2)] + 1)
                    empty_chunks(("pT", t, i), g, probT[:, t % 2])
                if t == T - 1:
                    act.wait_ge(r_pr, 1)
                    act.activation(pr[:, :, :], pr[:, :, :], ACT.Exp).then_inc(r_act, 1)
                empty_stage(("y", t), xf[:, t, :], stage_bank(("y", t))[:, 0:P])
                if t + LAG_T < T:
                    exps(t + LAG_T)
                if t < FC:
                    w_hi_part(0, t)
                if t in ROUTE_AT:
                    if ROUTE_AT[t] == "logits":
                        empty_stage(("logits", 0), lg[:, :, :], logits_of(0))
                    else:
                        empty_xfT(0)
            act.preload_act_table(ACT.Silu)

            def experts(e, first, last):
                if not first:
                    hi_part(2 * FC * e - 1, (2 * FC - 1) % HB)
                act.activation(b1_now[:, :], b13T[:, 0, bass.ds(FC * e, FC)], ACT.Copy).then_inc(b1_ok, 1)
                for j, (c, _) in enumerate(FIRST_ORDER if first else ORDER):
                    u = 2 * FC * e + j
                    act.wait_ge(g1a, u + 1)
                    act.wait_ge(gate_ok, u + 1)
                    if j == 0:
                        act.wait_ge(b1_ok, e + 1)
                    act.activation(silu[:, j % 2, :], psum[:, j % 2, :], ACT.Silu,
                                   bias=b1_now[:, c:c + 1]).then_inc(silu_ok, 1)
                    if j > 0:
                        hi_part(u - 1, (j - 1) % HB)
                    if first and j == 1:
                        empty_xfT(1)
                    elif first and j == 2:
                        empty_stage(("logits", 1), logit[1][:, :, :], logits_of(1))
                    elif first and j in (4, 6):
                        b = (j - 4) // 2
                        empty_stage(("combT", b), combT[:, b * BANK:(b + 1) * BANK], stage_bank(("combT", b))[0:E, :])
                    if j in (1, 3) and not first:
                        w_hi_part(e, FC // 2 + j // 2)
                    elif j in (5, 7) and not last:
                        w_hi_part(e + 1, j // 2 - FC // 2, past=(FIRST_DONE[j // 2 - FC // 2] if first else None))

            def hi_part(u, slot_h):
                act.wait_ge(gate_ok, u + 3)
                act.wait_ge(g2_ok, u + 1)
                act.activation(h_hi[:, slot_h, :], h[:, slot_h % 2, :], ACT.Copy).then_inc(hhi_ok, 1)

            experts(0, True, False)
            with act.Fori(1, E - 1) as e:
                experts(e, False, False)
            experts(E - 1, False, True)
            hi_part(2 * FC * E - 1, (2 * FC - 1) % HB)

        @block.vector
        def _(dve):
            def copy_bank(n, kind, i):
                bank = psum[:, n % PB, :]
                dve.wait_ge(pre_mm, n + 1)
                par, g = h_groups[i]
                dve.wait_ge(pre_act, empties(n, "a"))
                for b in range(B):
                    ins = dve.scalar_tensor_tensor(
                        out=head_cols(g_lo, b, par, g), in0=bank_heads(bank, b, g), scalar=SCALE,
                        in1=head_cols(g_hi, b, par, g).bitcast(F32), op0=ALU.mult, op1=ALU.subtract)
                ins.then_inc(pre_dve, 1)

            stat, normed = [0], [0]

            def ln_stats(src, tiles):
                for t in tiles:
                    dve.bn_stats(stats[:, t, :], src[:, t, :]).then_inc(ln_stat, 1)
                    stat[0] += 1
                for k, t in enumerate(tiles):
                    dve.wait_ge(ln_stat, stat[0] - len(tiles) + k + 1)
                    dve.bn_aggr(mv[:, t, :], stats[:, t, :]).then_inc(ln_mv, 1)

            def ln_apply(n, src, dst, tiles):
                dve.wait_ge(ln_pool, 2 * n + 2)
                for t in tiles:
                    dve.tensor_scalar(dst[:, t, :], src[:, t, :], mv[:, t, 0:1], rstd[:, t:t + 1],
                                      ALU.subtract, ALU.mult).then_inc(ln_out, 1)

            first, second = range(0, TB), range(TB, T)
            dve.wait_ge(ld["x0"], 16)
            ln_stats(x_sb, first)
            dve.wait_ge(ld["x1"], 16)
            ln_stats(x_sb, second)
            ln_apply(0, x_sb, xn, first)
            dve.wait_ge(ln_out, TB)
            ln_stats(xn, first)
            ln_apply(1, x_sb, xn, second)
            dve.wait_ge(ln_out, 2 * TB)
            ln_stats(xn, second)
            ln_apply(2, xn, xn, first)
            ln_apply(3, xn, xn, second)
            for n, (kind, i) in enumerate(plan):
                if kind == "g":
                    copy_bank(n, kind, i)
                elif kind == "xnT":
                    half = slice(i * TB, (i + 1) * TB)
                    dve.wait_ge(pre_act, empties(n, "a"))
                    dve.tensor_tensor(xn_lo[:, half, :], xnT[:, half, :], xn_hi[:, half, :].bitcast(F32),
                                      ALU.subtract).then_inc(s_dve, 1)

            def scores(t):
                return psum[:, 3 * (t % 2):3 * (t % 2) + 3, :].rearrange("p a n -> p (a n)")[:, 0:HM].rearrange("p (h m) -> p h m", h=H)

            def heads(t):
                return prob[:, t % NP_, :].rearrange("p (h m) -> p h m", h=H)

            chain = [B]

            def sums(t):
                dve.wait_ge(s_exp, t + 1)
                dve.tensor_reduce(rowsum[:, t, :], heads(t), AX.X, ALU.add).then_inc(s_dve, 1)
                chain[0] += 1
                dve.wait_ge(s_dve, chain[0])
                dve.reciprocal(rowsum[:, t, :], rowsum[:, t, :]).then_inc(s_rcp, 1)

            for t in range(T):
                dve.wait_ge(s_mm, t + 1)
                dve.tensor_reduce(negmax[:, t, :], scores(t), AX.X, ALU.max, negate=True).then_inc(s_dve, 1)
                chain[0] += 1
                dve.wait_ge(s_dve, chain[0])
                if t >= NP_:
                    dve.wait_ge(st_mm, slot[("pT", t - NP_, len(pt_groups) - 1)] + 1)
                dve.tensor_tensor(heads(t), scores(t),
                                  negmax[:, t, :].rearrange("p (h o) -> p h o", o=1).broadcast_to([P, H, M]),
                                  ALU.add).then_inc(s_sub, 1)
                if t - LAG_T - 1 >= 0:
                    dve.wait_ge(x2_ok, t - LAG_T)
                    ln_stats(x2, [t - LAG_T - 1])
                if t >= 1:
                    sums(t - 1)
            ln_apply(4, x2, xf, first)
            sums(T - 1)
            dve.wait_ge(ld["router"], 32)
            dve.wait_ge(const_ok, 4)
            route = [0]

            def link(ins):
                ins.then_inc(r_dve, 1)
                route[0] += 1
                dve.wait_ge(r_dve, route[0])

            def over_e(a):
                return a.rearrange("p (t o) -> p t o", o=1).broadcast_to([P, TB, E])

            def xf_lo_part(b):
                half = slice(b * BANK, (b + 1) * BANK)
                dve.wait_ge(xf_hi_ok, b + 1)
                dve.wait_ge(st_free, slot[("xfT", b)] + 1)
                dve.tensor_tensor(xf_lo[:, half], xfT[:, half], xf_hi[:, half].bitcast(F32), ALU.subtract).then_inc(xf_lo_ok, 1)

            def shift_logits(b):
                lgb = logit[b]
                dve.wait_ge(st_free, slot[("logits", b)] + 1)
                link(dve.tensor_tensor(lgb[:, :, :], lgb[:, :, :],
                                       bg_sb[:, :].rearrange("p (o e) -> p o e", o=1).broadcast_to([P, TB, E]), ALU.add))
                link(dve.tensor_reduce(red[:, :], lgb[:, :, :], AX.X, ALU.max))
                dve.tensor_tensor(expo[b][:, :, :], lgb[:, :, :], over_e(red[:, :]), ALU.subtract).then_inc(r_pr, 1)

            def rank_logits(b):
                lgb = logit[b]
                for t in range(TB):
                    other = lgb[:, t, :].rearrange("p (o e) -> p o e", o=1).broadcast_to([P, E, E])
                    me = lgb[:, t, :].rearrange("p (e o) -> p e o", o=1).broadcast_to([P, E, E])
                    dve.tensor_tensor(cmp_a[:, t * E:(t + 1) * E, :], other, me, ALU.is_gt).then_inc(r_dve, 1)
                    dve.tensor_tensor(cmp_b[:, t * E:(t + 1) * E, :], other, me, ALU.is_equal).then_inc(r_dve, 1)
                    route[0] += 2
                dve.wait_ge(r_dve, route[0])
                low4 = lower[:, :, :].rearrange("p e f -> p (e f)").rearrange("p (o n) -> p o n", o=1).broadcast_to([P, TB, E * E])
                b4 = cmp_b[:, :, :].rearrange("p (t e) f -> p t (e f)", t=TB)
                link(dve.tensor_tensor(b4, b4, low4, ALU.mult))
                link(dve.tensor_tensor(cmp_a[:, :, :], cmp_a[:, :, :], cmp_b[:, :, :], ALU.add))
                link(dve.tensor_reduce(rank[:, :, :].rearrange("p t e -> p (t e)"), cmp_a[:, :, :], AX.X, ALU.add))
                link(dve.tensor_scalar(rank[:, :, :], rank[:, :, :], 2.0, None, ALU.is_lt))

            def combine_weights(b):
                prb = expo[b]
                dve.wait_ge(r_exp1 if b else r_act, 1)
                link(dve.tensor_reduce(red[:, :], prb[:, :, :], AX.X, ALU.add))
                link(dve.reciprocal(red[:, :], red[:, :]))
                link(dve.tensor_tensor(prb[:, :, :], prb[:, :, :], over_e(red[:, :]), ALU.mult))
                link(dve.tensor_tensor(prb[:, :, :], prb[:, :, :], rank[:, :, :], ALU.mult))
                link(dve.tensor_reduce(red[:, :], prb[:, :, :], AX.X, ALU.add))
                link(dve.tensor_scalar(red[:, :], red[:, :], 1e-6, None, ALU.add))
                link(dve.reciprocal(red[:, :], red[:, :]))
                dve.tensor_tensor(comb[:, b * TB:(b + 1) * TB, :], prb[:, :, :], over_e(red[:, :]), ALU.mult).then_inc(comb_ok, 1)

            def late_stats(t):
                dve.wait_ge(x2_ok, t + 1)
                ln_stats(x2, [t])

            late_stats(T - 4)
            xf_lo_part(0)
            late_stats(T - 3)
            shift_logits(0)
            rank_logits(0)
            late_stats(T - 2)
            combine_weights(0)
            late_stats(T - 1)

            dve.sem_inc(gate_ok, 2)
            dve.sem_inc(y_used, 2)

            def lo_part(u, j):
                dve.wait_ge(hhi_ok, u + 1)
                dve.tensor_tensor(h_lo[:, j % HB, :], h[:, j % 2, :], h_hi[:, j % HB, :].bitcast(F32),
                                  ALU.subtract).then_inc(hlo_ok, 1)

            def combine(e, b):
                dve.wait_ge(g2_ok, 2 * FC * e + (HB + 2 * FC - 1 + b))
                dve.wait_ge(acc_ok, 2 * e + (b + 1))
                dve.scalar_tensor_tensor(out=y_c[:, b, :], in0=psum[:, 4 + b, :], scalar=b2T[:, bass.ds(e, 1)],
                                         in1=cb[:, bass.ds(e, 1), b * BANK:(b + 1) * BANK].rearrange("p a n -> p (a n)"),
                                         op0=ALU.add, op1=ALU.mult).then_inc(y_used, 1)

            def gate(e, j, c):
                u = 2 * FC * e + j
                if not isinstance(u, int) or u >= 2:
                    dve.wait_ge(hlo_ok, u - 1)
                dve.wait_ge(g1b, u + 1)
                dve.wait_ge(silu_ok, u + 1)
                dve.scalar_tensor_tensor(out=h[:, j % 2, :], in0=psum[:, 2 + j % 2, :],
                                         scalar=b13T[:, 1, bass.ds(FC * e + c, 1)], in1=silu[:, j % 2, :],
                                         op0=ALU.add, op1=ALU.mult).then_inc(gate_ok, 1)

            def experts(e, first):
                between = {0: lambda: ln_apply(5, x2, xf, second), 1: lambda: xf_lo_part(1), 2: lambda: shift_logits(1),
                           3: lambda: rank_logits(1), 4: lambda: combine_weights(1)} if first else {}
                for j, (c, _) in enumerate(FIRST_ORDER if first else ORDER):
                    gate(e, j, c)
                    if j > 0 or not first:
                        lo_part(2 * FC * e + j - 1, (j - 1) % HB)
                    if j in between:
                        between[j]()
                    if 0 < j <= B and not first:
                        combine(e - 1, j - 1)

            experts(0, True)
            dve.wait_ge(cb_first, 16 * B)
            experts(1, False)
            dve.wait_ge(cb_ok, 16 * (E - 1) * B)
            with dve.Fori(2, E) as e:
                experts(e, False)
            lo_part(2 * FC * E - 1, (2 * FC - 1) % HB)
            for b in range(B):
                combine(E - 1, b)

            for b in range(B):
                dve.wait_ge(o_mm, b + 1)
                half = slice(b * TB, (b + 1) * TB)
                dve.tensor_tensor(xn[:, half, :], x2[:, half, :], psum[:, 6 + b, :].rearrange("p (t d) -> p t d", d=P),
                                  ALU.add).then_inc(o_ok, 1)

        @block.tensor
        def _(pe):
            def mm3(dst, w_h, w_l, m_h, m_l):
                pe.matmul(dst, w_h, m_h, start=True, stop=False)
                pe.matmul(dst, w_l, m_h, start=False, stop=False)
                return pe.matmul(dst, w_h, m_l, start=False, stop=True)

            pe.wait_ge(ident_ok, 1)
            def open_pre(n):
                if n >= PB:
                    for who, s in (("a", pre_act), ("d", pre_dve)):
                        if who in emptied_by[plan[n - PB][0]]:
                            pe.wait_ge(s, empties(n - PB, who))
                return psum[:, n % PB, :]

            def both_parities(banks, g, done, left, right):
                for k, pair in enumerate(g):
                    for par in range(2):
                        r = slice(DH * par, DH * par + DH)
                        ins = pe.matmul(banks[par][:, k * B * M:(k + 1) * B * M], left[r, pair, :], right[r, pair, :],
                                        start=True, stop=True)
                        if k == len(g) - 1:
                            ins.then_inc(done, 1)

            for n, (kind, i) in enumerate(plan):
                if kind == "g":
                    par, g = h_groups[i]
                    if i == 0:
                        pe.wait_ge(pre_act, empties(place[("wqT", PAIRS // 4 - 1)], "a"))
                    if par == 0:
                        both_parities([open_pre(n), open_pre(n + 1)], g, pre_mm, wqT, kT)
                    continue
                bank = open_pre(n)
                if kind == "ctxT":
                    pe.wait_ge(ld["ctx"], 16)
                    for b in range(B):
                        ins = pe.transpose(bank[:, b * M:(b + 1) * M], ctx_sb[:, b, :], ident[0:M, 0:M])
                elif kind == "vecs":
                    pe.wait_ge(ld["vecs"], 80)
                    ins = pe.transpose(bank[:, 0:VECS], vec_rows[:, :], ident[0:VECS, 0:VECS])
                elif kind == "wqT":
                    if i == 0:
                        pe.wait_ge(ld["wq"], 16)
                    for k in range(4):
                        pair = 4 * i + k
                        ins = pe.transpose(bank[:, k * P:(k + 1) * P], wq_sb[:, pair * P:(pair + 1) * P], ident[:, :])
                elif kind == "xnT":
                    pe.wait_ge(ln_out, 2 * T - TB + TB * i)
                    for k in range(TB):
                        ins = pe.transpose(bank[:, k * P:(k + 1) * P], xn[:, TB * i + k, :], ident[:, :])
                else:
                    if i == 0:
                        pe.wait_ge(ld["wk"], 16)
                        pe.wait_ge(pre_act, 1)
                    for k, pair in enumerate(kv_groups[i]):
                        ins = pe.matmul(bank[:, k * B * M:(k + 1) * B * M], wkv_sb[:, pair * P:(pair + 1) * P],
                                        ctxT[:, :], start=True, stop=True)
                ins.then_inc(pre_mm, 1)

            def score_mm(t):
                b = t // TB
                if t % TB == 0:
                    pe.wait_ge(s_dve, b + 1)
                if t >= 2:
                    pe.wait_ge(s_sub, t - 1)
                for k in range(3):
                    cols = slice(k * BANK, min((k + 1) * BANK, HM))
                    ins = mm3(psum[:, 3 * (t % 2) + k, 0:cols.stop - cols.start], xn_hi[:, t, :], xn_lo[:, t, :],
                              g_hi[:, b, cols], g_lo[:, b, cols])
                ins.then_inc(s_mm, 1)

            def open_stage(key):
                if slot[key] >= 2:
                    pe.wait_ge(st_free, slot[key] - 1)
                return stage_bank(key)

            pe.wait_ge(pre_act, empties(len(plan) - 1, "a"))
            pe.wait_ge(pre_dve, empties(len(plan) - 1, "d"))
            score_mm(0)
            score_mm(1)
            pe.wait_ge(ld["wv"], 16)
            for i, g in enumerate(kv_groups):
                bank = open_stage(("vT", i))
                for k, pair in enumerate(g):
                    ins = pe.matmul(bank[:, k * B * M:(k + 1) * B * M],
                                    wkv_sb[:, INNER + pair * P:INNER + (pair + 1) * P], ctxT[:, :], start=True, stop=True)
                ins.then_inc(st_mm, 1)
            pe.wait_ge(ld["wout"], 16)
            for i, (par, g) in enumerate(h_groups):
                if par == 0:
                    pe.wait_ge(st_free, slot[("vT", i // 2)] + 1)
                    both_parities([open_stage(("voT", i)), open_stage(("voT", i + 1))], g, st_mm, wout_sb, vT)
            score_mm(2)
            for i, (b, g) in enumerate(vo_groups):
                if i == 0:
                    pe.wait_ge(st_free, slot[("voT", len(h_groups) - 1)] + 1)
                bank = open_stage(("vo", i))
                for k, c in enumerate(g):
                    ins = pe.transpose(bank[0:rows(c), k * P:(k + 1) * P], voT[:, b, c * P:c * P + rows(c)], ident[:, :])
                ins.then_inc(st_mm, 1)

            def router_mm(kind, b):
                bank = open_stage((kind, b))
                if kind == "xfT":
                    pe.wait_ge(ln_out, 2 * T + TB * (b + 1))
                elif kind == "logits":
                    pe.wait_ge(st_free, slot[("xfT", b)] + 1)
                else:
                    pe.wait_ge(comb_ok, b + 1)
                for k in range(TB):
                    t = TB * b + k
                    if kind == "xfT":
                        ins = pe.transpose(bank[:, k * P:(k + 1) * P], xf[:, t, :], ident[:, :])
                    elif kind == "logits":
                        ins = pe.matmul(bank[:, k * E:(k + 1) * E], xfT[:, t * P:(t + 1) * P], wg_sb[:, :],
                                        start=True, stop=True)
                    else:
                        ins = pe.transpose(bank[0:E, k * P:(k + 1) * P], comb[:, t, :], ident[:, :])
                ins.then_inc(st_mm, 1)

            pe.wait_ge(ld["router"], 32)
            for t in range(T):
                pe.wait_ge(s_norm, t + 1)
                for i, g in enumerate(pt_groups):
                    if i == len(pt_groups) - 1 and t + LAG_T < T:
                        score_mm(t + LAG_T)
                    bank = open_stage(("pT", t, i))
                    for k, c in enumerate(g):
                        ins = pe.transpose(bank[0:rows(c), k * P:(k + 1) * P], prob[:, t % NP_, c * P:c * P + rows(c)], ident[:, :])
                    ins.then_inc(st_mm, 1)
                bank = open_stage(("y", t))
                for c in range(CH):
                    if c % 4 == 0:
                        pe.wait_ge(st_free, slot[("pT", t, c // 4)] + 1)
                    ins = pe.matmul(bank[:, 0:P], probT[0:rows(c), t % 2, c, :], vo[0:rows(c), t // TB, c, :],
                                    start=(c == 0), stop=(c == CH - 1))
                ins.then_inc(st_mm, 1)
                if t in ROUTE_AT:
                    router_mm(ROUTE_AT[t], 0)

            pe.sem_inc(g2_ok, HB)
            LAG = 3

            def up(e, j, order=ORDER):
                c, b = order[j]
                u = 2 * FC * e + j
                half = slice(b * BANK, (b + 1) * BANK)
                pe.wait_ge(w_split, FC * e + (c + 1))
                pe.wait_ge(gate_ok, u + 1)
                mm3(psum[:, j % 2, :], w_hi[:, c, 0, :], w_lo[:, c, 0, :], xf_hi[:, half], xf_lo[:, half]).then_inc(g1a, 1)
                mm3(psum[:, 2 + j % 2, :], w_hi[:, c, 1, :], w_lo[:, c, 1, :], xf_hi[:, half], xf_lo[:, half]).then_inc(g1b, 1)

            def down(e, j, order=ORDER):
                c, b = order[j]
                u = 2 * FC * e + j
                pe.wait_ge(hlo_ok, u + 1)
                if c == 0:
                    pe.wait_ge(y_used, 2 * e + (b + 1))
                dst = psum[:, 4 + b, :]
                pe.matmul(dst, w_hi[:, c, 2, :], h_hi[:, j % HB, :], start=(c == 0), stop=False)
                pe.matmul(dst, w_lo[:, c, 2, :], h_hi[:, j % HB, :], start=False, stop=False)
                pe.matmul(dst, w_hi[:, c, 2, :], h_lo[:, j % HB, :], start=False, stop=(c == FC - 1)).then_inc(g2_ok, 1)

            def steady(e):
                for j in range(2 * FC):
                    k = j + LAG
                    up(e + k // (2 * FC), k % (2 * FC)) if k >= 2 * FC else up(e, k)
                    down(e, j)

            pe.wait_ge(xf_lo_ok, 1)
            up(0, 0, FIRST_ORDER)
            up(0, 1, FIRST_ORDER)
            router_mm("xfT", 1)
            up(0, 2, FIRST_ORDER)
            router_mm("logits", 1)
            pe.wait_ge(xf_lo_ok, 2)
            for j in range(2 * FC):
                k = j + LAG
                up(1, k - 2 * FC) if k >= 2 * FC else up(0, k, FIRST_ORDER)
                down(0, j, FIRST_ORDER)
                if j in (1, 4):
                    router_mm("combT", j // 4)
            with pe.Fori(1, E - 1) as e:
                steady(e)
            for j in range(2 * FC):
                if j + LAG < 2 * FC:
                    up(E - 1, j + LAG)
                down(E - 1, j)
            for b in range(B):
                pe.wait_ge(acc_ok, 2 * E + b + 1)
                for k in range(TB):
                    ins = pe.transpose(psum[:, 6 + b, k * P:(k + 1) * P], acc[:, b, k * P:(k + 1) * P], ident[:, :])
                ins.then_inc(o_mm, 1)


_INS = ['x', 'ctx_1024', 'L0_xattn_W_q', 'L0_xattn_W_kv', 'L0_xattn_W_out', 'L0_xattn_ln_gamma', 'L0_xattn_ln_beta',
        'L0_ffn_Wg', 'L0_ffn_bg', 'L0_ffn_W1', 'L0_ffn_b1', 'L0_ffn_W3', 'L0_ffn_b3', 'L0_ffn_W2', 'L0_ffn_b2']
_OUTS = [((2, 512, 128), 'float32')]


def kernel(**inputs):
    import numpy as _np
    import concourse.bacc as _bacc
    from concourse import mybir as _mybir
    from concourse.bass_utils import run_bass_kernel_spmd as _run

    nc = _bacc.Bacc("TRN2", target_bir_lowering=False, num_devices=1)
    arrays, args = {}, []
    for name in _INS:
        a = _np.ascontiguousarray(inputs[name])
        arrays[f"in_{name}_dram"] = a
        args.append(nc.dram_tensor(f"in_{name}_dram", a.shape, _mybir.dt.from_np(a.dtype), kind="ExternalInput").ap())
    for i, (shape, dtype) in enumerate(_OUTS):
        dt = _mybir.dt.from_np(_np.dtype(dtype))
        args.append(nc.dram_tensor(f"out_{i}_dram", shape, dt, kind="ExternalOutput").ap())
    build(nc, *args)
    r = _run(nc, [arrays], core_ids=[0])
    got = tuple(r.results[0][f"out_{i}_dram"] for i in range(len(_OUTS)))
    return got[0]
```

```python
from contextlib import ExitStack

import concourse.bass as bass
from concourse import mybir

F32 = mybir.dt.float32
F32R = mybir.dt.float32r
ALU = mybir.AluOpType
ACT = mybir.ActivationFunctionType
AX = mybir.AxisListType

P = 128
BANK = 512
EPS = 1e-5
HALF_ROOT = -0.5
E_BASE = 2.718281828459045


def build(nc, x, ctx_in, w_q, w_kv, w_out, gamma, beta, w_g, b_g, w_1, b_1, w_3, b_3, w_2, b_2, out):
    B, S, D = x.shape
    M = ctx_in.shape[1]
    INNER = w_q.shape[1]
    DH = 64
    H = INNER // DH
    PAIRS = H // 2
    E = w_1.shape[0]
    FF = w_1.shape[2]
    FC = FF // P
    T = B * S // P
    TB = S // P
    HM = H * M
    CH = -(-HM // P)
    N = B * S
    SCALE = DH ** -0.5
    assert D == P and TB * P == BANK and E == 8

    ctx = ExitStack()
    with ctx:
        def sb(name, shape, dt=F32):
            return ctx.enter_context(nc.sbuf_tensor(name, shape, dt))

        def sem(name):
            return ctx.enter_context(nc.semaphore(name))

        psum = ctx.enter_context(nc.psum_tensor("psum", [P, 8, BANK], F32))

        ident = sb("ident", [P, P])
        neg_half = sb("neg_half", [P, T])
        euler = sb("euler", [P, TB, E])
        x_sb = sb("x_sb", [P, T, P])
        ctx_sb = sb("ctx_sb", [M, B, P])
        wq_sb = sb("wq_sb", [P, INNER])
        wkv_sb = sb("wkv_sb", [P, 2 * INNER])
        wout_sb = sb("wout_sb", [P, PAIRS, P])
        wg_sb = sb("wg_sb", [P, E])
        bg_sb = sb("bg_sb", [P, E])
        VECS = 2 * E * FC + E + 2
        vec_rows = sb("vec_rows", [VECS, P])
        vecs = sb("vecs", [P, VECS])
        b13T = vecs[:, 0:2 * E * FC].rearrange("p (a n) -> p a n", a=2)
        b2T = vecs[:, 2 * E * FC:2 * E * FC + E]
        gamma_sb = vecs[:, VECS - 2:VECS - 1]
        beta_sb = vecs[:, VECS - 1:VECS]
        ctxT = sb("ctxT", [P, B * M])
        wqT = sb("wqT", [P, PAIRS, P])
        kT = sb("kT", [P, PAIRS, B * M])
        vT = sb("vT", [P, PAIRS, B * M])
        g_hi = sb("g_hi", [P, B, HM], F32R)
        g_lo = sb("g_lo", [P, B, HM], F32R)
        voT = sb("voT", [P, B, HM])
        vo = sb("vo", [P, B, CH, P])
        stats = sb("stats", [P, T, 6])
        mv = sb("mv", [P, T, 2])
        rstd = sb("rstd", [P, T])
        xn = sb("xn", [P, T, P])
        xnT = sb("xnT", [P, T, P])
        xn_hi = sb("xn_hi", [P, T, P], F32R)
        xn_lo = sb("xn_lo", [P, T, P], F32R)
        NP_ = 4
        prob = sb("prob", [P, NP_, HM])
        probT = sb("probT", [P, 2, CH, P])
        negmax = sb("negmax", [P, T, H])
        rowsum = sb("rowsum", [P, T, H])
        x2 = sb("x2", [P, T, P])
        xf = sb("xf", [P, T, P])
        xfT = sb("xfT", [P, N])
        xf_hi = sb("xf_hi", [P, N], F32R)
        xf_lo = sb("xf_lo", [P, N], F32R)
        lg = sb("lg", [P, TB, E])
        pr = sb("pr", [P, TB, E])
        red = sb("red", [P, TB])
        cmp_a = sb("cmp_a", [P, TB * E, E])
        cmp_b = sb("cmp_b", [P, TB * E, E])
        lower = sb("lower", [P, E, E])
        rank = sb("rank", [P, TB, E])
        comb = sb("comb", [P, T, E])
        logit = [lg, sb("lg1", [P, TB, E])]
        expo = [pr, sb("pr1", [P, TB, E])]
        combT = sb("combT", [E, N])
        comb_dram = nc.dram_tensor("comb_scratch", [E, N], F32, kind="Internal")
        cb = sb("cb", [P, E, N])
        b1_now = sb("b1_now", [P, FC])
        w_raw = sb("w_raw", [P, FC, 3, P])
        w_hi = sb("w_hi", [P, FC, 3, P], F32R)
        w_lo = sb("w_lo", [P, FC, 3, P], F32R)
        HB = 4
        old_prob = prob[:, :, :].rearrange("p n c -> p (n c)")
        silu, h, y_c = (old_prob[:, 2 * BANK * i:2 * BANK * (i + 1)].rearrange("p (n c) -> p n c", n=2) for i in range(3))
        h_hi, h_lo = (g[:, :, :].rearrange("p b c -> p (b c)")[:, 0:HB * BANK].rearrange("p (n c) -> p n c", n=HB)
                      for g in (g_hi, g_lo))
        acc = sb("acc", [P, 2, BANK])

        ld = {n: sem("ld_" + n) for n in ("x0", "x1", "ctx", "wq", "wk", "wv", "wout", "router", "vecs")}
        ident_ok = sem("ident_ok")
        ident_z = sem("ident_z")
        const_ok = sem("const_ok")
        pre_mm = sem("pre_mm")
        pre_act = sem("pre_act")
        pre_dve = sem("pre_dve")
        ln_stat = sem("ln_stat")
        ln_mv = sem("ln_mv")
        ln_pool = sem("ln_pool")
        ln_out = sem("ln_out")
        xn_ok = [sem(f"xn_ok{b}") for b in range(B)]
        s_mm = sem("s_mm")
        s_dve = sem("s_dve")
        s_sub = sem("s_sub")
        s_exp = sem("s_exp")
        s_rcp = sem("s_rcp")
        s_norm = sem("s_norm")
        st_mm = sem("st_mm")
        st_free = sem("st_free")
        x2_ok = sem("x2_ok")
        xf_hi_ok = sem("xf_hi_ok")
        xf_lo_ok = sem("xf_lo_ok")
        r_act = sem("r_act")
        r_exp1 = sem("r_exp1")
        r_dve = sem("r_dve")
        r_pr = sem("r_pr")
        comb_ok = sem("comb_ok")
        comb_st = sem("comb_st")
        cb_first = [sem(f"cb_first{b}") for b in range(B)]
        cb_ok = sem("cb_ok")
        raw_ok = [sem(f"raw_ok{c}") for c in range(FC)]
        hi_w = sem("hi_w")
        w_split = sem("w_split")
        b1_ok = sem("b1_ok")
        g1a = sem("g1a")
        g1b = sem("g1b")
        silu_ok = sem("silu_ok")
        gate_ok = sem("gate_ok")
        hhi_ok = sem("hhi_ok")
        hlo_ok = sem("hlo_ok")
        g2_ok = sem("g2_ok")
        y_used = sem("y_used")
        acc_z = sem("acc_z")
        acc_last = sem("acc_last")
        acc_ok = sem("acc_ok")
        o_mm = sem("o_mm")
        o_ok = sem("o_ok")
        stored = sem("stored")

        PER = BANK // (B * M)
        kv_groups = [range(i, min(i + PER, PAIRS)) for i in range(0, PAIRS, PER)]
        h_groups = [(par, g) for g in kv_groups for par in range(2)]

        def head_cols(a, par, g):
            return a[:, :, (par * PAIRS + g.start) * M:(par * PAIRS + g.stop) * M]

        def bank_heads(bank, g):
            return bank[:, 0:len(g) * B * M].rearrange("p (b n) -> p b n", b=B)

        plan = [("ctxT", 0)] + [("kT", i) for i in range(len(kv_groups))] + [("wqT", i) for i in range(PAIRS // 4)]
        plan += [("vecs", 0)]
        for i in range(len(h_groups)):
            plan += [("g", i)] + ([("xnT", i // 2)] if i % 2 and i // 2 < B else [])
        emptied_by = {"ctxT": "a", "vecs": "a", "wqT": "a", "kT": "a", "g": "ad", "xnT": "a"}
        PB = 8

        def empties(n, who):
            return sum(who in emptied_by[k] for k, _ in plan[:n + 1])

        place = {key: n for n, key in enumerate(plan)}
        assert len(h_groups) >= 2 * B

        LAG_T = 3
        ORDER = [(j // 2, j % 2) for j in range(2 * FC)]
        FIRST_ORDER = [(0, 0), (1, 0), (2, 0), (3, 0), (2, 1), (3, 1), (0, 1), (1, 1)]
        LAST_ORDER = [(0, 0), (0, 1), (1, 0), (1, 1), (2, 0), (3, 0), (2, 1), (3, 1)]
        assert FC == 4
        FIRST_SPLIT = [2, 3, 0, 1]

        def order_of(e):
            return {0: FIRST_ORDER, E - 1: LAST_ORDER}.get(e, ORDER) if isinstance(e, int) else ORDER

        def split_count(e, c):
            return FIRST_SPLIT.index(c) + 1 if isinstance(e, int) and e == 0 else FC * e + (c + 1)

        def split_in(parts, tokens_part, e, c):
            if isinstance(e, int) and e == 0 and c < 2:
                return tokens_part[:, 3 * c:3 * c + 3, :]
            return parts[:, c, :, :]

        halves = [range(0, TB), range(TB, T)]
        norms = [halves[0], halves[0], halves[1], halves[1], halves[0], range(TB, T - 1), range(T - 1, T)]
        normed_by = [sum(len(g) for g in norms[:n + 1]) for n in range(len(norms))]

        vo_groups = [(b, range(i, min(i + 4, CH))) for b in range(B) for i in range(0, CH, 4)]
        stage = [("vT", i) for i in range(len(kv_groups))] + [("voT", i) for i in range(len(h_groups))]
        stage += [("vo", i) for i in range(len(vo_groups))]
        pt_groups = [range(i, min(i + 4, CH)) for i in range(0, CH, 4)]
        for t in range(T):
            stage += [("pT", t, i) for i in range(len(pt_groups))] + ([("logits", 0)] if t == T - 2 else []) + [("y", t)]
            if t == T - 3:
                stage += [("xfT", 0)]
        stage += [("xfT", 1), ("logits", 1), ("combT", 0), ("combT", 1)]
        slot = {key: n for n, key in enumerate(stage)}

        def stage_bank(key):
            return psum[:, 7 - slot[key] % 2, :]

        def rows(c):
            return min(P, HM - c * P)

        RANKED = 2 + 2 * TB

        block = ctx.enter_context(nc.Block())

        @block.sync
        def _(sp):
            x_v = x.rearrange("b (t p) d -> p (b t) d", p=P)
            sp.dma_start(x_sb[:, 0:TB, :], x_v[:, 0:TB, :]).then_inc(ld["x0"], 16)
            sp.dma_start(wkv_sb[:, 0:INNER], w_kv[:, 0:INNER]).then_inc(ld["wk"], 16)
            row = 0
            for src in (b_1.rearrange("e (c p) -> (e c) p", p=P), b_3.rearrange("e (c p) -> (e c) p", p=P), b_2[:, :],
                        gamma.rearrange("(o p) -> o p", o=1), beta.rearrange("(o p) -> o p", o=1)):
                sp.dma_start(vec_rows[row:row + src.shape[0], :], src).then_inc(ld["vecs"], 16)
                row += src.shape[0]
            sp.dma_start(wkv_sb[:, INNER:2 * INNER], w_kv[:, INNER:2 * INNER]).then_inc(ld["wv"], 16)
            sp.dma_start(wout_sb[:, :, :], w_out.rearrange("(c p) d -> p c d", p=P)).then_inc(ld["wout"], 16)
            sp.dma_start(wg_sb[:, :], w_g[:, :]).then_inc(ld["router"], 16)
            sp.dma_start(bg_sb[:, :], b_g.partition_broadcast(P)).then_inc(ld["router"], 16)

            def load_expert(e):
                for c in range(FC):
                    cols = slice(c * P, (c + 1) * P)
                    if not isinstance(e, int) or e > 0:
                        sp.wait_ge(w_split, split_count(e - 1, c))
                    sp.dma_start(w_raw[:, c, 0, :], w_1[bass.ds(e, 1), :, cols].rearrange("a k n -> (a k) n")).then_inc(raw_ok[c], 16)
                    sp.dma_start(w_raw[:, c, 1, :], w_3[bass.ds(e, 1), :, cols].rearrange("a k n -> (a k) n")).then_inc(raw_ok[c], 16)
                    sp.dma_start(w_raw[:, c, 2, :], w_2[bass.ds(e, 1), cols, :].rearrange("a k n -> (a k) n")).then_inc(raw_ok[c], 16)

            load_expert(0)
            load_expert(1)
            for b in range(B):
                half = slice(b * BANK, (b + 1) * BANK)
                sp.wait_ge(st_free, slot[("combT", b)] + 1)
                sp.dma_start(comb_dram[:, half], combT[:, half]).then_inc(comb_st, 16)
                sp.wait_ge(comb_st, 16 * (b + 1))
                for e in range(E):
                    sp.dma_start(cb[:, e, half], comb_dram[e:e + 1, half].partition_broadcast(P)).then_inc(cb_ok if e else cb_first[b], 16)
            with sp.Fori(2, E) as e:
                load_expert(e)
            out_v = out.rearrange("b (t p) d -> p (b t) d", p=P)
            for b in range(B):
                sp.wait_ge(o_ok, b + 1)
                sp.dma_start(out_v[:, b * TB:(b + 1) * TB, :], xn[:, b * TB:(b + 1) * TB, :]).then_inc(stored, 16)
            sp.wait_ge(stored, 16 * B)

        @block.gpsimd
        def _(pool):
            pool.memset(ident[:, :], 0.0).then_inc(ident_z, 1)
            pool.wait_ge(ident_z, 1)
            pool.affine_select(out=ident[:, :], in_=ident[:, :], compare_op=ALU.not_equal, fill=1.0,
                               base=0, pattern=[[-1, P]], channel_multiplier=1).then_inc(ident_ok, 1)
            pool.memset(neg_half[:, :], HALF_ROOT).then_inc(const_ok, 1)
            pool.memset(lower[:, :, :], 1.0).then_inc(const_ok, 1)
            pool.wait_ge(const_ok, 2)
            pool.affine_select(out=lower[:, :, :], in_=lower[:, :, :], compare_op=ALU.is_gt, fill=0.0,
                               base=0, pattern=[[1, E], [-1, E]], channel_multiplier=0).then_inc(const_ok, 1)
            pool.memset(euler[:, :, :], E_BASE).then_inc(const_ok, 1)
            pool.memset(acc[:, :, :], 0.0).then_inc(acc_z, 1)

            def rstd_step(n):
                tiles = slice(norms[n].start, norms[n].stop)
                pool.wait_ge(ln_mv, normed_by[n])
                pool.tensor_scalar(rstd[:, tiles], mv[:, tiles, 1], EPS, None, ALU.add).then_inc(ln_pool, 1)
                pool.wait_ge(ln_pool, 2 * n + 1)
                pool.tensor_tensor(rstd[:, tiles], rstd[:, tiles], neg_half[:, tiles], ALU.pow).then_inc(ln_pool, 1)

            for n in range(4):
                rstd_step(n)
            second = slice(TB, T)
            pool.wait_ge(pre_act, empties(place[("xnT", 1)], "a"))
            pool.tensor_tensor(xn_lo[:, second, :], xnT[:, second, :], xn_hi[:, second, :].bitcast(F32),
                               ALU.subtract).then_inc(xn_ok[1], 1)

            def lo_part(e, c):
                pool.wait_ge(hi_w, split_count(e, c))
                pool.tensor_tensor(split_in(w_lo, xn_lo, e, c), w_raw[:, c, :, :], split_in(w_hi, xn_hi, e, c).bitcast(F32),
                                   ALU.subtract).then_inc(w_split, 1)

            def add_x(t):
                pool.wait_ge(st_free, slot[("y", t)] + 1)
                pool.tensor_tensor(x2[:, t, :], x_sb[:, t, :], xf[:, t, :], ALU.add).then_inc(x2_ok, 1)

            for t in range(T):
                if t >= LAG_T:
                    add_x(t - LAG_T)
                if t - LAG_T == TB - 1:
                    rstd_step(4)
                if 4 <= t < 6:
                    lo_part(0, FIRST_SPLIT[t - 4])
                pool.wait_ge(s_rcp, t + 1)
                pool.tensor_tensor(prob[:, t % NP_, :].rearrange("p (h m) -> p h m", h=H),
                                   prob[:, t % NP_, :].rearrange("p (h m) -> p h m", h=H),
                                   rowsum[:, t, :].rearrange("p (h o) -> p h o", o=1).broadcast_to([P, H, M]),
                                   ALU.mult).then_inc(s_norm, 1)
            lo_part(0, FIRST_SPLIT[2])
            for t in range(T - LAG_T, T - 1):
                add_x(t)
            rstd_step(5)
            lo_part(0, FIRST_SPLIT[3])
            add_x(T - 1)
            rstd_step(6)
            lo_part(1, 0)
            pool.wait_ge(r_pr, 2)
            pool.tensor_tensor(expo[1][:, :, :], euler[:, :, :], expo[1][:, :, :], ALU.pow).then_inc(r_exp1, 1)

            pool.wait_ge(acc_z, 1)
            pool.sem_inc(acc_ok, 2)

            def accumulate(e, halves=range(B)):
                for b in halves:
                    pool.wait_ge(y_used, 2 * e + (b + 3))
                    pool.wait_ge(acc_ok, 2 * e + (b + 1))
                    pool.tensor_tensor(acc[:, b, :], acc[:, b, :], y_c[:, b, :], ALU.add).then_inc(acc_ok, 1)

            for c in range(1, FC // 2):
                lo_part(1, c)
            with pool.Fori(1, E - 1) as e:
                for c in range(FC // 2, FC):
                    lo_part(e, c)
                accumulate(e - 1)
                for c in range(FC // 2):
                    lo_part(e + 1, c)
            for c in range(FC // 2, FC):
                lo_part(E - 1, c)
            accumulate(E - 2)
            accumulate(E - 1, [0])

        @block.scalar
        def _(act):
            act.dma_start(ctx_sb[:, :, :], ctx_in.rearrange("b m d -> m b d")).then_inc(ld["ctx"], 16)
            act.dma_start(x_sb[:, TB:T, :], x.rearrange("b (t p) d -> p (b t) d", p=P)[:, TB:T, :]).then_inc(ld["x1"], 16)
            act.dma_start(wq_sb[:, :], w_q[:, :]).then_inc(ld["wq"], 16)

            for n, (kind, i) in enumerate(plan):
                bank = psum[:, n % PB, :]
                act.wait_ge(pre_mm, n + 1)
                if kind == "ctxT":
                    ins = act.activation(ctxT[:, :], bank[:, 0:B * M], ACT.Copy)
                elif kind == "vecs":
                    ins = act.activation(vecs[:, :], bank[:, 0:VECS], ACT.Copy)
                elif kind == "wqT":
                    ins = act.activation(wqT[:, 4 * i:4 * i + 4, :], bank.rearrange("p (a d) -> p a d", d=P), ACT.Copy)
                elif kind == "kT":
                    g = kv_groups[i]
                    ins = act.activation(kT[:, g.start:g.stop, :],
                                         bank[:, 0:len(g) * B * M].rearrange("p (a m) -> p a m", a=len(g)), ACT.Copy)
                elif kind == "xnT":
                    if i == 0:
                        act.wait_ge(pre_act, place[("vecs", 0)] + 1)
                    for dst in (xn_hi, xnT):
                        ins = act.activation(dst[:, TB * i:TB * i + TB, :], bank.rearrange("p (a d) -> p a d", d=P),
                                             ACT.Identity, scale=gamma_sb, bias=beta_sb)
                else:
                    par, g = h_groups[i]
                    ins = act.activation(head_cols(g_hi, par, g), bank_heads(bank, g), ACT.Copy, scale=SCALE)
                ins.then_inc(pre_act, 1)

            def logits_of(b):
                return stage_bank(("logits", b))[:, 0:TB * E].rearrange("p (t e) -> p t e", e=E)

            def w_hi_part(e, c):
                act.wait_ge(raw_ok[c], 48 * e + 48)
                if isinstance(e, int) and e == 0:
                    if c < 2:
                        act.wait_ge(s_mm, T)
                elif not isinstance(e, int) or e > 1 or c >= 2:
                    act.wait_ge(g2_ok, HB + 2 * FC * e + (2 * c + 2 - 2 * FC))
                act.activation(split_in(w_hi, xn_hi, e, c), w_raw[:, c, :, :], ACT.Copy).then_inc(hi_w, 1)

            def empty_stage(key, dst, src):
                act.wait_ge(st_mm, slot[key] + 1)
                act.activation(dst, src, ACT.Copy).then_inc(st_free, 1)

            def empty_xfT(b):
                half = slice(b * BANK, (b + 1) * BANK)
                act.wait_ge(st_mm, slot[("xfT", b)] + 1)
                act.activation(xf_hi[:, half], stage_bank(("xfT", b)), ACT.Copy).then_inc(xf_hi_ok, 1)
                act.activation(xfT[:, half], stage_bank(("xfT", b)), ACT.Copy).then_inc(st_free, 1)

            def exps(t):
                act.wait_ge(s_sub, t + 1)
                act.activation(prob[:, t % NP_, :], prob[:, t % NP_, :], ACT.Exp).then_inc(s_exp, 1)

            for i, g in enumerate(kv_groups):
                empty_stage(("vT", i), vT[:, g.start:g.stop, :],
                            stage_bank(("vT", i))[:, 0:len(g) * B * M].rearrange("p (a m) -> p a m", a=len(g)))
            exps(0)
            for i, (par, g) in enumerate(h_groups):
                act.wait_ge(st_mm, slot[("voT", i)] + 1)
                act.activation(head_cols(voT, par, g), bank_heads(stage_bank(("voT", i)), g), ACT.Copy).then_inc(st_free, 1)
                if i == 3:
                    exps(1)

            def empty_chunks(key, g, dst):
                full = [c for c in g if rows(c) == P]
                src = stage_bank(key).rearrange("p (a d) -> p a d", d=P)
                ins = act.activation(dst[:, full[0]:full[-1] + 1, :], src[:, 0:len(full), :], ACT.Copy)
                if len(full) < len(g):
                    c = g[-1]
                    ins = act.activation(dst[0:rows(c), c, :], src[0:rows(c), len(full), :], ACT.Copy)
                ins.then_inc(st_free, 1)

            for i, (b, g) in enumerate(vo_groups):
                act.wait_ge(st_mm, slot[("vo", i)] + 1)
                empty_chunks(("vo", i), g, vo[:, b])
            exps(2)
            for t in range(T):
                for i, g in enumerate(pt_groups):
                    act.wait_ge(st_mm, slot[("pT", t, i)] + 1)
                    if i == 0 and t >= 2:
                        act.wait_ge(st_mm, slot[("y", t - 2)] + 1)
                    empty_chunks(("pT", t, i), g, probT[:, t % 2])
                if t == T - 2:
                    empty_stage(("logits", 0), lg[:, :, :], logits_of(0))
                if t < T - 1:
                    empty_stage(("y", t), xf[:, t, :], stage_bank(("y", t))[:, 0:P])
                if t + LAG_T < T:
                    exps(t + LAG_T)
                if t == T - 3:
                    empty_xfT(0)
                if t in (1, 2, 5, 6):
                    w_hi_part(0, FIRST_SPLIT[{1: 0, 2: 1, 5: 2, 6: 3}[t]])
                if t == T - 2:
                    act.wait_ge(r_pr, 1)
                    act.activation(pr[:, :, :], pr[:, :, :], ACT.Exp).then_inc(r_act, 1)
                    act.wait_ge(r_act, 1)
                    act.preload_act_table(ACT.Silu)

            def experts(e, first, last):
                if not first:
                    hi_part(2 * FC * e - 1, (2 * FC - 1) % HB)
                act.activation(b1_now[:, :], b13T[:, 0, bass.ds(FC * e, FC)], ACT.Copy).then_inc(b1_ok, 1)
                for j, (c, _) in enumerate(order_of(e)):
                    u = 2 * FC * e + j
                    act.wait_ge(g1a, u + 1)
                    act.wait_ge(gate_ok, u + 1)
                    if j == 0:
                        act.wait_ge(b1_ok, e + 1)
                    act.activation(silu[:, j % 2, :], psum[:, j % 2, :], ACT.Silu,
                                   bias=b1_now[:, c:c + 1]).then_inc(silu_ok, 1)
                    if first and j == 0:
                        empty_stage(("y", T - 1), xf[:, T - 1, :], stage_bank(("y", T - 1))[:, 0:P])
                    if first and j == 2:
                        empty_xfT(1)
                    if j > 0:
                        hi_part(u - 1, (j - 1) % HB)
                    if first and j == 3:
                        empty_stage(("logits", 1), logit[1][:, :, :], logits_of(1))
                    elif first and j == 6:
                        empty_combT(0)
                    if first and j in (3, 5):
                        w_hi_part(1, j // 2 - 1)
                    elif j in (1, 3) and not first:
                        w_hi_part(e, FC // 2 + j // 2)
                    elif j in (5, 7) and not first and not last:
                        w_hi_part(e + 1, j // 2 - FC // 2)

            def empty_combT(b):
                empty_stage(("combT", b), combT[:, b * BANK:(b + 1) * BANK], stage_bank(("combT", b))[0:E, :])

            def hi_part(u, slot_h):
                act.wait_ge(gate_ok, u + 3)
                act.wait_ge(g2_ok, u + 1)
                act.activation(h_hi[:, slot_h, :], h[:, slot_h % 2, :], ACT.Copy).then_inc(hhi_ok, 1)

            experts(0, True, False)
            empty_combT(1)
            with act.Fori(1, E - 1) as e:
                experts(e, False, False)
            experts(E - 1, False, True)
            hi_part(2 * FC * E - 1, (2 * FC - 1) % HB)

        @block.vector
        def _(dve):
            def copy_bank(n, kind, i):
                bank = psum[:, n % PB, :]
                dve.wait_ge(pre_mm, n + 1)
                par, g = h_groups[i]
                dve.wait_ge(pre_act, empties(n, "a"))
                dve.scalar_tensor_tensor(
                    out=head_cols(g_lo, par, g), in0=bank_heads(bank, g), scalar=SCALE,
                    in1=head_cols(g_hi, par, g).bitcast(F32), op0=ALU.mult, op1=ALU.subtract).then_inc(pre_dve, 1)

            stat = [0]

            def ln_stats(src, tiles):
                for t in tiles:
                    dve.bn_stats(stats[:, t, :], src[:, t, :]).then_inc(ln_stat, 1)
                    stat[0] += 1
                for k, t in enumerate(tiles):
                    dve.wait_ge(ln_stat, stat[0] - len(tiles) + k + 1)
                    dve.bn_aggr(mv[:, t, :], stats[:, t, :]).then_inc(ln_mv, 1)

            def ln_apply(n, src, dst):
                dve.wait_ge(ln_pool, 2 * n + 2)
                for t in norms[n]:
                    dve.tensor_scalar(dst[:, t, :], src[:, t, :], mv[:, t, 0:1], rstd[:, t:t + 1],
                                      ALU.subtract, ALU.mult).then_inc(ln_out, 1)

            dve.wait_ge(ld["x0"], 16)
            ln_stats(x_sb, halves[0])
            ln_apply(0, x_sb, xn)
            dve.wait_ge(ln_out, TB)
            ln_stats(xn, halves[0])
            dve.wait_ge(ld["x1"], 16)
            ln_stats(x_sb, halves[1])
            ln_apply(1, xn, xn)
            ln_apply(2, x_sb, xn)
            dve.wait_ge(ln_out, 3 * TB)
            ln_stats(xn, halves[1])
            for n, (kind, i) in enumerate(plan):
                if kind == "g":
                    copy_bank(n, kind, i)
                    if i == 1:
                        ln_apply(3, xn, xn)
                elif kind == "xnT" and i == 0:
                    half = slice(0, TB)
                    dve.wait_ge(pre_act, empties(n, "a"))
                    dve.tensor_tensor(xn_lo[:, half, :], xnT[:, half, :], xn_hi[:, half, :].bitcast(F32),
                                      ALU.subtract).then_inc(xn_ok[0], 1)

            def scores(t):
                return psum[:, 3 * (t % 2):3 * (t % 2) + 3, :].rearrange("p a n -> p (a n)")[:, 0:HM].rearrange("p (h m) -> p h m", h=H)

            def heads(t):
                return prob[:, t % NP_, :].rearrange("p (h m) -> p h m", h=H)

            chain = [0]

            def sums(t):
                dve.wait_ge(s_exp, t + 1)
                dve.tensor_reduce(rowsum[:, t, :], heads(t), AX.X, ALU.add).then_inc(s_dve, 1)
                chain[0] += 1
                dve.wait_ge(s_dve, chain[0])
                dve.reciprocal(rowsum[:, t, :], rowsum[:, t, :]).then_inc(s_rcp, 1)

            for t in range(T):
                dve.wait_ge(s_mm, t + 1)
                dve.tensor_reduce(negmax[:, t, :], scores(t), AX.X, ALU.max, negate=True).then_inc(s_dve, 1)
                chain[0] += 1
                dve.wait_ge(s_dve, chain[0])
                if t >= NP_:
                    dve.wait_ge(st_mm, slot[("pT", t - NP_, len(pt_groups) - 1)] + 1)
                dve.tensor_tensor(heads(t), scores(t),
                                  negmax[:, t, :].rearrange("p (h o) -> p h o", o=1).broadcast_to([P, H, M]),
                                  ALU.add).then_inc(s_sub, 1)
                if t - LAG_T - 1 >= 0:
                    dve.wait_ge(x2_ok, t - LAG_T)
                    ln_stats(x2, [t - LAG_T - 1])
                if t >= 1:
                    sums(t - 1)
            ln_apply(4, x2, xf)
            sums(T - 1)
            dve.wait_ge(s_sub, T)
            dve.sem_inc(gate_ok, 2)
            dve.sem_inc(y_used, 2)
            dve.wait_ge(ld["router"], 32)
            dve.wait_ge(const_ok, 4)
            route = [0]

            def link(ins):
                ins.then_inc(r_dve, 1)
                route[0] += 1
                dve.wait_ge(r_dve, route[0])

            def over_e(a):
                return a.rearrange("p (t o) -> p t o", o=1).broadcast_to([P, TB, E])

            def xf_lo_part(b):
                half = slice(b * BANK, (b + 1) * BANK)
                dve.wait_ge(xf_hi_ok, b + 1)
                dve.wait_ge(st_free, slot[("xfT", b)] + 1)
                dve.tensor_tensor(xf_lo[:, half], xfT[:, half], xf_hi[:, half].bitcast(F32), ALU.subtract).then_inc(xf_lo_ok, 1)

            def shift_logits(b):
                lgb = logit[b]
                dve.wait_ge(st_free, slot[("logits", b)] + 1)
                link(dve.tensor_tensor(lgb[:, :, :], lgb[:, :, :],
                                       bg_sb[:, :].rearrange("p (o e) -> p o e", o=1).broadcast_to([P, TB, E]), ALU.add))
                link(dve.tensor_reduce(red[:, :], lgb[:, :, :], AX.X, ALU.max))
                dve.tensor_tensor(expo[b][:, :, :], lgb[:, :, :], over_e(red[:, :]), ALU.subtract).then_inc(r_pr, 1)

            def rank_logits(b):
                lgb = logit[b]
                for t in range(TB):
                    other = lgb[:, t, :].rearrange("p (o e) -> p o e", o=1).broadcast_to([P, E, E])
                    me = lgb[:, t, :].rearrange("p (e o) -> p e o", o=1).broadcast_to([P, E, E])
                    dve.tensor_tensor(cmp_a[:, t * E:(t + 1) * E, :], other, me, ALU.is_gt).then_inc(r_dve, 1)
                    dve.tensor_tensor(cmp_b[:, t * E:(t + 1) * E, :], other, me, ALU.is_equal).then_inc(r_dve, 1)
                    route[0] += 2
                dve.wait_ge(r_dve, route[0])
                low4 = lower[:, :, :].rearrange("p e f -> p (e f)").rearrange("p (o n) -> p o n", o=1).broadcast_to([P, TB, E * E])
                b4 = cmp_b[:, :, :].rearrange("p (t e) f -> p t (e f)", t=TB)
                link(dve.tensor_tensor(b4, b4, low4, ALU.mult))
                link(dve.tensor_tensor(cmp_a[:, :, :], cmp_a[:, :, :], cmp_b[:, :, :], ALU.add))
                link(dve.tensor_reduce(rank[:, :, :].rearrange("p t e -> p (t e)"), cmp_a[:, :, :], AX.X, ALU.add))
                link(dve.tensor_scalar(rank[:, :, :], rank[:, :, :], 2.0, None, ALU.is_lt))

            def combine_weights(b):
                prb = expo[b]
                dve.wait_ge(r_exp1 if b else r_act, 1)
                link(dve.tensor_reduce(red[:, :], prb[:, :, :], AX.X, ALU.add))
                link(dve.reciprocal(red[:, :], red[:, :]))
                link(dve.tensor_tensor(prb[:, :, :], prb[:, :, :], over_e(red[:, :]), ALU.mult))
                link(dve.tensor_tensor(prb[:, :, :], prb[:, :, :], rank[:, :, :], ALU.mult))
                link(dve.tensor_reduce(red[:, :], prb[:, :, :], AX.X, ALU.add))
                link(dve.tensor_scalar(red[:, :], red[:, :], 1e-6, None, ALU.add))
                link(dve.reciprocal(red[:, :], red[:, :]))
                dve.tensor_tensor(comb[:, b * TB:(b + 1) * TB, :], prb[:, :, :], over_e(red[:, :]), ALU.mult).then_inc(comb_ok, 1)

            def late_stats(t):
                dve.wait_ge(x2_ok, t + 1)
                ln_stats(x2, [t])

            shift_logits(0)
            xf_lo_part(0)
            late_stats(T - 4)
            late_stats(T - 3)
            rank_logits(0)
            late_stats(T - 2)
            combine_weights(0)

            def lo_part(u, j):
                dve.wait_ge(hhi_ok, u + 1)
                dve.tensor_tensor(h_lo[:, j % HB, :], h[:, j % 2, :], h_hi[:, j % HB, :].bitcast(F32),
                                  ALU.subtract).then_inc(hlo_ok, 1)

            def combine(e, b):
                dve.wait_ge(g2_ok, 2 * FC * e + (HB + 1 + max(j for j, (_, half) in enumerate(order_of(e)) if half == b)))
                dve.wait_ge(acc_ok, 2 * e + (b + 1))
                dve.scalar_tensor_tensor(out=y_c[:, b, :], in0=psum[:, 4 + b, :], scalar=b2T[:, bass.ds(e, 1)],
                                         in1=cb[:, bass.ds(e, 1), b * BANK:(b + 1) * BANK].rearrange("p a n -> p (a n)"),
                                         op0=ALU.add, op1=ALU.mult).then_inc(y_used, 1)

            def gate(e, j, c):
                u = 2 * FC * e + j
                if not isinstance(u, int) or u >= 2:
                    dve.wait_ge(hlo_ok, u - 1)
                dve.wait_ge(g1b, u + 1)
                dve.wait_ge(silu_ok, u + 1)
                dve.scalar_tensor_tensor(out=h[:, j % 2, :], in0=psum[:, 2 + j % 2, :],
                                         scalar=b13T[:, 1, bass.ds(FC * e + c, 1)], in1=silu[:, j % 2, :],
                                         op0=ALU.add, op1=ALU.mult).then_inc(gate_ok, 1)

            def finish_norm():
                ln_apply(5, x2, xf)
                late_stats(T - 1)
                ln_apply(6, x2, xf)

            def experts(e, first):
                between = {0: finish_norm, 2: lambda: xf_lo_part(1), 3: lambda: shift_logits(1),
                           4: lambda: rank_logits(1), 7: lambda: combine_weights(1)} if first else {}
                for j, (c, _) in enumerate(order_of(e)):
                    gate(e, j, c)
                    if j > 0 or not first:
                        lo_part(2 * FC * e + j - 1, (j - 1) % HB)
                    if j in between:
                        between[j]()
                    if 0 < j <= B and not first:
                        if isinstance(e, int) and e == 1:
                            dve.wait_ge(cb_first[j - 1], 16)
                        combine(e - 1, j - 1)

            experts(0, True)
            experts(1, False)
            dve.wait_ge(cb_ok, 16 * (E - 1) * B)
            with dve.Fori(2, E - 1) as e:
                experts(e, False)
            experts(E - 1, False)
            lo_part(2 * FC * E - 1, (2 * FC - 1) % HB)
            for b in range(B):
                combine(E - 1, b)
            dve.wait_ge(y_used, 2 * E + 2)
            dve.tensor_tensor(acc[:, 1, :], acc[:, 1, :], y_c[:, 1, :], ALU.add).then_inc(acc_last, 1)

            for b in range(B):
                dve.wait_ge(o_mm, b + 1)
                half = slice(b * TB, (b + 1) * TB)
                dve.tensor_tensor(xn[:, half, :], x2[:, half, :], psum[:, 6 + b, :].rearrange("p (t d) -> p t d", d=P),
                                  ALU.add).then_inc(o_ok, 1)

        @block.tensor
        def _(pe):
            def mm3(dst, w_h, w_l, m_h, m_l):
                pe.matmul(dst, w_h, m_h, start=True, stop=False)
                pe.matmul(dst, w_l, m_h, start=False, stop=False)
                return pe.matmul(dst, w_h, m_l, start=False, stop=True)

            def open_pre(n):
                if n >= PB:
                    for who, s in (("a", pre_act), ("d", pre_dve)):
                        if who in emptied_by[plan[n - PB][0]]:
                            pe.wait_ge(s, empties(n - PB, who))
                return psum[:, n % PB, :]

            def both_parities(banks, g, done, left, right):
                for k, pair in enumerate(g):
                    for par in range(2):
                        r = slice(DH * par, DH * par + DH)
                        ins = pe.matmul(bank_heads(banks[par], g)[:, :, k * M:(k + 1) * M], left[r, pair, :],
                                        right[r, pair, :].rearrange("p (b m) -> p b m", b=B),
                                        start=True, stop=True)
                        if k == len(g) - 1:
                            ins.then_inc(done, 1)

            pe.wait_ge(ident_ok, 1)
            def warm_up(n):
                for k in range(n):
                    pe.transpose(psum[:, PB - 1, 0:P], ident[:, :], ident[:, :])

            warm_up(10)
            for n, (kind, i) in enumerate(plan):
                if kind == "g":
                    par, g = h_groups[i]
                    if i == 0:
                        pe.wait_ge(pre_act, empties(place[("wqT", PAIRS // 4 - 1)], "a"))
                    if par == 0:
                        both_parities([open_pre(n), open_pre(n + 1)], g, pre_mm, wqT, kT)
                    continue
                bank = open_pre(n)
                if kind == "ctxT":
                    pe.wait_ge(ld["ctx"], 16)
                    for b in range(B):
                        ins = pe.transpose(bank[:, b * M:(b + 1) * M], ctx_sb[:, b, :], ident[0:M, 0:M])
                    ins.then_inc(pre_mm, 1)
                    warm_up(5)
                    continue
                elif kind == "vecs":
                    pe.wait_ge(ld["vecs"], 80)
                    ins = pe.transpose(bank[:, 0:VECS], vec_rows[:, :], ident[0:VECS, 0:VECS])
                elif kind == "wqT":
                    if i == 0:
                        pe.wait_ge(ld["wq"], 16)
                    for k in range(4):
                        pair = 4 * i + k
                        ins = pe.transpose(bank[:, k * P:(k + 1) * P], wq_sb[:, pair * P:(pair + 1) * P], ident[:, :])
                elif kind == "xnT":
                    pe.wait_ge(ln_out, 2 * TB * (i + 1))
                    for k in range(TB):
                        ins = pe.transpose(bank[:, k * P:(k + 1) * P], xn[:, TB * i + k, :], ident[:, :])
                else:
                    if i == 0:
                        pe.wait_ge(ld["wk"], 16)
                        pe.wait_ge(pre_act, 1)
                    for k, pair in enumerate(kv_groups[i]):
                        ins = pe.matmul(bank[:, k * B * M:(k + 1) * B * M], wkv_sb[:, pair * P:(pair + 1) * P],
                                        ctxT[:, :], start=True, stop=True)
                ins.then_inc(pre_mm, 1)

            def score_mm(t):
                b = t // TB
                if t % TB == 0:
                    pe.wait_ge(xn_ok[b], 1)
                if t >= 2:
                    pe.wait_ge(s_sub, t - 1)
                for k in range(3):
                    cols = slice(k * BANK, min((k + 1) * BANK, HM))
                    ins = mm3(psum[:, 3 * (t % 2) + k, 0:cols.stop - cols.start], xn_hi[:, t, :], xn_lo[:, t, :],
                              g_hi[:, b, cols], g_lo[:, b, cols])
                ins.then_inc(s_mm, 1)

            def open_stage(key):
                if slot[key] >= 2:
                    pe.wait_ge(st_free, slot[key] - 1)
                return stage_bank(key)

            def value_T(i):
                bank = open_stage(("vT", i))
                for k, pair in enumerate(kv_groups[i]):
                    ins = pe.matmul(bank[:, k * B * M:(k + 1) * B * M],
                                    wkv_sb[:, INNER + pair * P:INNER + (pair + 1) * P], ctxT[:, :], start=True, stop=True)
                ins.then_inc(st_mm, 1)

            def value_out(i):
                pe.wait_ge(st_free, slot[("vT", i // 2)] + 1)
                both_parities([open_stage(("voT", i)), open_stage(("voT", i + 1))], h_groups[i][1], st_mm, wout_sb, vT)

            def emptied(n):
                pe.wait_ge(pre_act, empties(n, "a"))
                pe.wait_ge(pre_dve, empties(n, "d"))

            pe.wait_ge(ld["wv"], 16)
            emptied(max(n for n in range(len(plan)) if n % PB == 7))
            value_T(0)
            emptied(len(plan) - 1)
            score_mm(0)
            for i in range(1, len(kv_groups)):
                value_T(i)
            score_mm(1)
            pe.wait_ge(ld["wout"], 16)
            value_out(0)
            score_mm(2)
            for i in range(2, len(h_groups), 2):
                value_out(i)
            pe.wait_ge(st_free, slot[("voT", len(h_groups) - 1)] + 1)
            for i, (b, g) in enumerate(vo_groups):
                bank = open_stage(("vo", i))
                for k, c in enumerate(g):
                    ins = pe.transpose(bank[0:rows(c), k * P:(k + 1) * P], voT[:, b, c * P:c * P + rows(c)], ident[:, :])
                ins.then_inc(st_mm, 1)

            def router_mm(kind, b):
                bank = open_stage((kind, b))
                if kind == "xfT":
                    pe.wait_ge(ln_out, 2 * T + TB * (b + 1))
                elif kind == "logits":
                    pe.wait_ge(st_free, slot[("xfT", b)] + 1)
                else:
                    pe.wait_ge(comb_ok, b + 1)
                for k in range(TB):
                    t = TB * b + k
                    if kind == "xfT":
                        ins = pe.transpose(bank[:, k * P:(k + 1) * P], xf[:, t, :], ident[:, :])
                    elif kind == "logits":
                        ins = pe.matmul(bank[:, k * E:(k + 1) * E], xfT[:, t * P:(t + 1) * P], wg_sb[:, :],
                                        start=True, stop=True)
                    else:
                        ins = pe.transpose(bank[0:E, k * P:(k + 1) * P], comb[:, t, :], ident[:, :])
                ins.then_inc(st_mm, 1)

            pe.wait_ge(ld["router"], 32)
            LAG = 3

            def up(e, j):
                c, b = order_of(e)[j]
                w_h, w_l = split_in(w_hi, xn_hi, e, c), split_in(w_lo, xn_lo, e, c)
                u = 2 * FC * e + j
                half = slice(b * BANK, (b + 1) * BANK)
                pe.wait_ge(w_split, split_count(e, c))
                pe.wait_ge(gate_ok, u + 1)
                mm3(psum[:, j % 2, :], w_h[:, 0, :], w_l[:, 0, :], xf_hi[:, half], xf_lo[:, half]).then_inc(g1a, 1)
                mm3(psum[:, 2 + j % 2, :], w_h[:, 1, :], w_l[:, 1, :], xf_hi[:, half], xf_lo[:, half]).then_inc(g1b, 1)

            def down(e, j):
                order = order_of(e)
                c, b = order[j]
                w_h, w_l = split_in(w_hi, xn_hi, e, c), split_in(w_lo, xn_lo, e, c)
                mine = [k for k, (_, half) in enumerate(order) if half == b]
                u = 2 * FC * e + j
                pe.wait_ge(hlo_ok, u + 1)
                if j == mine[0]:
                    pe.wait_ge(y_used, 2 * e + (b + 1))
                dst = psum[:, 4 + b, :]
                pe.matmul(dst, w_h[:, 2, :], h_hi[:, j % HB, :], start=(j == mine[0]), stop=False)
                pe.matmul(dst, w_l[:, 2, :], h_hi[:, j % HB, :], start=False, stop=False)
                pe.matmul(dst, w_h[:, 2, :], h_lo[:, j % HB, :], start=False, stop=(j == mine[-1])).then_inc(g2_ok, 1)

            def steady(e):
                for j in range(2 * FC):
                    k = j + LAG
                    up(e + k // (2 * FC), k % (2 * FC)) if k >= 2 * FC else up(e, k)
                    down(e, j)

            pe.wait_ge(ld["router"], 32)
            for t in range(T):
                pe.wait_ge(s_norm, t + 1)
                for i, g in enumerate(pt_groups):
                    if i == len(pt_groups) - 1:
                        if t + LAG_T < T:
                            score_mm(t + LAG_T)
                        elif t == T - 1:
                            pe.wait_ge(xf_lo_ok, 1)
                            up(0, 0)
                    bank = open_stage(("pT", t, i))
                    for k, c in enumerate(g):
                        ins = pe.transpose(bank[0:rows(c), k * P:(k + 1) * P], prob[:, t % NP_, c * P:c * P + rows(c)], ident[:, :])
                    ins.then_inc(st_mm, 1)
                if t == T - 2:
                    router_mm("logits", 0)
                bank = open_stage(("y", t))
                for c in range(CH):
                    if c % 4 == 0:
                        pe.wait_ge(st_free, slot[("pT", t, c // 4)] + 1)
                    ins = pe.matmul(bank[:, 0:P], probT[0:rows(c), t % 2, c, :], vo[0:rows(c), t // TB, c, :],
                                    start=(c == 0), stop=(c == CH - 1))
                ins.then_inc(st_mm, 1)
                if t == T - 3:
                    router_mm("xfT", 0)

            pe.sem_inc(g2_ok, HB)
            up(0, 1)
            up(0, 2)
            router_mm("xfT", 1)
            for j in range(2 * FC):
                k = j + LAG
                if k == FC:
                    pe.wait_ge(xf_lo_ok, 2)
                up(1, k - 2 * FC) if k >= 2 * FC else up(0, k)
                down(0, j)
                if j == 0:
                    router_mm("logits", 1)
                elif j in (3, 5):
                    router_mm("combT", j // 4)
            with pe.Fori(1, E - 1) as e:
                steady(e)
            for j in range(2 * FC):
                if j + LAG < 2 * FC:
                    up(E - 1, j + LAG)
                down(E - 1, j)
            for b in range(B):
                pe.wait_ge(*((acc_last, 1) if b else (acc_ok, 2 * E + 1)))
                for k in range(TB):
                    ins = pe.transpose(psum[:, 6 + b, k * P:(k + 1) * P], acc[:, b, k * P:(k + 1) * P], ident[:, :])
                ins.then_inc(o_mm, 1)


_INS = ['x', 'ctx_1024', 'L0_xattn_W_q', 'L0_xattn_W_kv', 'L0_xattn_W_out', 'L0_xattn_ln_gamma', 'L0_xattn_ln_beta',
        'L0_ffn_Wg', 'L0_ffn_bg', 'L0_ffn_W1', 'L0_ffn_b1', 'L0_ffn_W3', 'L0_ffn_b3', 'L0_ffn_W2', 'L0_ffn_b2']
_OUTS = [((2, 512, 128), 'float32')]


def kernel(**inputs):
    import numpy as _np
    import concourse.bacc as _bacc
    from concourse import mybir as _mybir
    from concourse.bass_utils import run_bass_kernel_spmd as _run

    nc = _bacc.Bacc("TRN2", target_bir_lowering=False, num_devices=1)
    arrays, args = {}, []
    for name in _INS:
        a = _np.ascontiguousarray(inputs[name])
        arrays[f"in_{name}_dram"] = a
        args.append(nc.dram_tensor(f"in_{name}_dram", a.shape, _mybir.dt.from_np(a.dtype), kind="ExternalInput").ap())
    for i, (shape, dtype) in enumerate(_OUTS):
        dt = _mybir.dt.from_np(_np.dtype(dtype))
        args.append(nc.dram_tensor(f"out_{i}_dram", shape, dt, kind="ExternalOutput").ap())
    build(nc, *args)
    r = _run(nc, [arrays], core_ids=[0])
    got = tuple(r.results[0][f"out_{i}_dram"] for i in range(len(_OUTS)))
    return got[0]
```

```python
from contextlib import ExitStack

import concourse.bass as bass
from concourse import mybir

F32 = mybir.dt.float32
F32R = mybir.dt.float32r
ALU = mybir.AluOpType
ACT = mybir.ActivationFunctionType
AX = mybir.AxisListType

P = 128
BANK = 512
EPS = 1e-5
HALF_ROOT = -0.5
E_BASE = 2.718281828459045


def build(nc, x, ctx_in, w_q, w_kv, w_out, gamma, beta, w_g, b_g, w_1, b_1, w_3, b_3, w_2, b_2, out):
    B, S, D = x.shape
    M = ctx_in.shape[1]
    INNER = w_q.shape[1]
    DH = 64
    H = INNER // DH
    PAIRS = H // 2
    E = w_1.shape[0]
    FF = w_1.shape[2]
    FC = FF // P
    T = B * S // P
    TB = S // P
    HM = H * M
    CH = -(-HM // P)
    N = B * S
    SCALE = DH ** -0.5
    assert D == P and TB * P == BANK and E == 8

    ctx = ExitStack()
    with ctx:
        def sb(name, shape, dt=F32):
            return ctx.enter_context(nc.sbuf_tensor(name, shape, dt))

        def sem(name):
            return ctx.enter_context(nc.semaphore(name))

        psum = ctx.enter_context(nc.psum_tensor("psum", [P, 8, BANK], F32))

        ident = sb("ident", [P, P])
        neg_half = sb("neg_half", [P, T])
        euler = sb("euler", [P, TB, E])
        x_sb = sb("x_sb", [P, T, P])
        ctx_sb = sb("ctx_sb", [M, B, P])
        wq_sb = sb("wq_sb", [P, INNER])
        wkv_sb = sb("wkv_sb", [P, 2 * INNER])
        wout_sb = sb("wout_sb", [P, PAIRS, P])
        wg_sb = sb("wg_sb", [P, E])
        bg_sb = sb("bg_sb", [P, E])
        VECS = 2 * E * FC + E + 2
        vec_rows = sb("vec_rows", [VECS, P])
        vecs = sb("vecs", [P, VECS])
        b13T = vecs[:, 0:2 * E * FC].rearrange("p (a n) -> p a n", a=2)
        b2T = vecs[:, 2 * E * FC:2 * E * FC + E]
        gamma_sb = vecs[:, VECS - 2:VECS - 1]
        beta_sb = vecs[:, VECS - 1:VECS]
        ctxT = sb("ctxT", [P, B * M])
        wqT = sb("wqT", [P, PAIRS, P])
        kT = sb("kT", [P, PAIRS, B * M])
        vT = sb("vT", [P, PAIRS, B * M])
        g_hi = sb("g_hi", [P, B, HM], F32R)
        g_lo = sb("g_lo", [P, B, HM], F32R)
        voT = sb("voT", [P, B, HM])
        vo = sb("vo", [P, B, CH, P])
        stats = sb("stats", [P, T, 6])
        mv = sb("mv", [P, T, 2])
        rstd = sb("rstd", [P, T])
        xn = sb("xn", [P, T, P])
        xnT = sb("xnT", [P, T, P])
        xn_hi = sb("xn_hi", [P, T, P], F32R)
        xn_lo = sb("xn_lo", [P, T, P], F32R)
        NP_ = 4
        prob = sb("prob", [P, NP_, HM])
        probT = sb("probT", [P, 2, CH, P])
        negmax = sb("negmax", [P, T, H])
        rowsum = sb("rowsum", [P, T, H])
        x2 = sb("x2", [P, T, P])
        xf = sb("xf", [P, T, P])
        xfT = sb("xfT", [P, N])
        xf_hi = sb("xf_hi", [P, N], F32R)
        xf_lo = sb("xf_lo", [P, N], F32R)
        lg = sb("lg", [P, TB, E])
        pr = sb("pr", [P, TB, E])
        red = sb("red", [P, TB])
        cmp_a = sb("cmp_a", [P, TB * E, E])
        cmp_b = sb("cmp_b", [P, TB * E, E])
        lower = sb("lower", [P, E, E])
        rank = sb("rank", [P, TB, E])
        comb = sb("comb", [P, T, E])
        logit = [lg, sb("lg1", [P, TB, E])]
        expo = [pr, sb("pr1", [P, TB, E])]
        combT = sb("combT", [E, N])
        comb_dram = nc.dram_tensor("comb_scratch", [E, N], F32, kind="Internal")
        cb = sb("cb", [P, E, N])
        b1_now = sb("b1_now", [P, FC])
        w_raw = sb("w_raw", [P, FC, 3, P])
        w_hi = sb("w_hi", [P, FC, 3, P], F32R)
        w_lo = sb("w_lo", [P, FC, 3, P], F32R)
        HB = 4
        old_prob = prob[:, :, :].rearrange("p n c -> p (n c)")
        silu, h, y_c = (old_prob[:, 2 * BANK * i:2 * BANK * (i + 1)].rearrange("p (n c) -> p n c", n=2) for i in range(3))
        h_hi, h_lo = (g[:, :, :].rearrange("p b c -> p (b c)")[:, 0:HB * BANK].rearrange("p (n c) -> p n c", n=HB)
                      for g in (g_hi, g_lo))
        acc = sb("acc", [P, 2, BANK])

        ld = {n: sem("ld_" + n) for n in ("x0", "x1", "ctx", "wq", "wk", "wv", "wout", "router", "vecs")}
        ident_ok = sem("ident_ok")
        ident_z = sem("ident_z")
        const_ok = sem("const_ok")
        pre_mm = sem("pre_mm")
        pre_act = sem("pre_act")
        pre_dve = sem("pre_dve")
        ln_stat = sem("ln_stat")
        ln_mv = sem("ln_mv")
        ln_pool = sem("ln_pool")
        ln_out = sem("ln_out")
        xn_ok = [sem(f"xn_ok{n}") for n in range(3)]
        xn_split = sem("xn_split")
        s_mm = sem("s_mm")
        s_dve = sem("s_dve")
        s_sub = sem("s_sub")
        s_exp = sem("s_exp")
        s_rcp = sem("s_rcp")
        s_norm = sem("s_norm")
        st_mm = sem("st_mm")
        st_free = sem("st_free")
        x2_ok = sem("x2_ok")
        xf_hi_ok = sem("xf_hi_ok")
        xf_lo_ok = sem("xf_lo_ok")
        r_act = sem("r_act")
        r_exp1 = sem("r_exp1")
        r_dve = sem("r_dve")
        r_pr = sem("r_pr")
        comb_ok = sem("comb_ok")
        comb_st = sem("comb_st")
        cb_first = [sem(f"cb_first{b}") for b in range(B)]
        cb_ok = sem("cb_ok")
        raw_ok = [sem(f"raw_ok{c}") for c in range(FC)]
        hi_w = sem("hi_w")
        w_split = sem("w_split")
        b1_ok = sem("b1_ok")
        g1a = sem("g1a")
        g1b = sem("g1b")
        silu_ok = sem("silu_ok")
        gate_ok = sem("gate_ok")
        hhi_ok = sem("hhi_ok")
        hlo_ok = sem("hlo_ok")
        g2_ok = sem("g2_ok")
        y_used = sem("y_used")
        acc_z = sem("acc_z")
        acc_last = sem("acc_last")
        acc_ok = sem("acc_ok")
        o_mm = sem("o_mm")
        o_ok = sem("o_ok")
        stored = sem("stored")

        PER = BANK // (B * M)
        kv_groups = [range(i, min(i + PER, PAIRS)) for i in range(0, PAIRS, PER)]
        h_groups = [(par, g) for g in kv_groups for par in range(2)]

        def head_cols(a, par, g):
            return a[:, :, (par * PAIRS + g.start) * M:(par * PAIRS + g.stop) * M]

        def bank_heads(bank, g):
            return bank[:, 0:len(g) * B * M].rearrange("p (b n) -> p b n", b=B)

        plan = [("ctxT", 0)] + [("kT", i) for i in range(len(kv_groups))] + [("wqT", i) for i in range(PAIRS // 4)]
        plan += [("vecs", 0)]
        plan += [("g", 0), ("g", 1), ("xnT", 0)] + [("g", i) for i in range(2, len(h_groups))] + [("xnT", 1)]
        xn_tiles = [range(0, 1), range(1, TB), range(TB, T)]
        emptied_by = {"ctxT": "a", "vecs": "a", "wqT": "a", "kT": "a", "g": "ad", "xnT": "a"}
        PB = 8

        def empties(n, who):
            return sum(who in emptied_by[k] for k, _ in plan[:n + 1])

        place = {key: n for n, key in enumerate(plan)}

        EARLY_VO = 2
        LEAD = 4
        LAG_T = 3
        ORDER = [(j // 2, j % 2) for j in range(2 * FC)]
        FIRST_ORDER = [(0, 0), (1, 0), (2, 0), (3, 0), (2, 1), (3, 1), (0, 1), (1, 1)]
        LAST_ORDER = [(0, 0), (0, 1), (1, 0), (1, 1), (2, 0), (3, 0), (2, 1), (3, 1)]
        assert FC == 4
        FIRST_SPLIT = [2, 0, 1, 3]
        SPLIT_AT = [3, 4, 5, 6]

        def order_of(e):
            return {0: FIRST_ORDER, E - 1: LAST_ORDER}.get(e, ORDER) if isinstance(e, int) else ORDER

        def split_count(e, c):
            return FIRST_SPLIT.index(c) + 1 if isinstance(e, int) and e == 0 else FC * e + (c + 1)

        def split_in(parts, tokens_part, e, c):
            if isinstance(e, int) and e == 0 and c < 2:
                return tokens_part[:, 3 * c:3 * c + 3, :]
            return parts[:, c, :, :]

        halves = [range(0, TB), range(TB, T)]
        norms = [halves[0], halves[0], halves[1], halves[1], halves[0], range(TB, T - 1), range(T - 1, T)]
        normed_by = [sum(len(g) for g in norms[:n + 1]) for n in range(len(norms))]

        vo_groups = [(b, range(i, min(i + 4, CH))) for b in range(B) for i in range(0, CH, 4)]
        stage = [("vT", i) for i in range(len(kv_groups))] + [("voT", i) for i in range(len(h_groups))]
        stage += [("xnT", 2)] + [("vo", i) for i in range(len(vo_groups))]
        pt_groups = [range(i, min(i + 4, CH)) for i in range(0, CH, 4)]
        for t in range(T):
            stage += [("pT", t, i) for i in range(len(pt_groups))]
            stage += ([("logits", 0)] if t == T - 2 else []) + [("y", t)]
            if t == T - 3:
                stage += [("xfT", 0)]
        stage += [("xfT", 1), ("logits", 1), ("combT", 0), ("combT", 1)]
        slot = {key: n for n, key in enumerate(stage)}

        OUT_PARTS = [slice(0, TB), slice(TB, TB + TB // 2), slice(TB + TB // 2, T)]

        def out_bank(tiles):
            n = OUT_PARTS.index(tiles)
            return psum[:, 3 + n, 0:(tiles.stop - tiles.start) * P].rearrange("p (t d) -> p t d", d=P)

        def y_bank(e, b):
            return psum[:, (4 if isinstance(e, int) and e == 0 else 6) + b, :]

        OWN = {("voT", 4): 3, ("voT", 5): 4,
               ("pT", T - 4, 2): 0, ("y", T - 4): 2, ("pT", T - 3, 2): 5, ("y", T - 3): 1, ("xfT", 0): 3,
               ("pT", T - 2, 2): 4, ("logits", 0): 0, ("y", T - 2): 1, ("pT", T - 1, 2): 5, ("y", T - 1): 4}
        bank_of, before, rotation = {}, {}, [7, 6]
        for key in stage:
            bank_of[key] = OWN[key] if key in OWN else rotation[0]
            if key not in OWN:
                rotation.reverse()
            before[key] = next((k for k in stage[:slot[key]][::-1] if bank_of[k] == bank_of[key]), None)

        def stage_bank(key):
            return psum[:, bank_of[key], :]

        def rows(c):
            return min(P, HM - c * P)

        block = ctx.enter_context(nc.Block())

        @block.sync
        def _(sp):
            x_v = x.rearrange("b (t p) d -> p (b t) d", p=P)
            sp.dma_start(x_sb[:, 0:TB, :], x_v[:, 0:TB, :]).then_inc(ld["x0"], 16)
            sp.dma_start(wkv_sb[:, 0:INNER], w_kv[:, 0:INNER]).then_inc(ld["wk"], 16)
            row = 0
            for src in (b_1.rearrange("e (c p) -> (e c) p", p=P), b_3.rearrange("e (c p) -> (e c) p", p=P), b_2[:, :],
                        gamma.rearrange("(o p) -> o p", o=1), beta.rearrange("(o p) -> o p", o=1)):
                sp.dma_start(vec_rows[row:row + src.shape[0], :], src).then_inc(ld["vecs"], 16)
                row += src.shape[0]
            sp.dma_start(wkv_sb[:, INNER:2 * INNER], w_kv[:, INNER:2 * INNER]).then_inc(ld["wv"], 16)
            sp.dma_start(wout_sb[:, :, :], w_out.rearrange("(c p) d -> p c d", p=P)).then_inc(ld["wout"], 16)
            sp.dma_start(wg_sb[:, :], w_g[:, :]).then_inc(ld["router"], 16)
            sp.dma_start(bg_sb[:, :], b_g.partition_broadcast(P)).then_inc(ld["router"], 16)

            def load_expert(e, chunks=range(FC)):
                for c in chunks:
                    cols = slice(c * P, (c + 1) * P)
                    if not isinstance(e, int) or e > 0:
                        sp.wait_ge(w_split, split_count(e - 1, c))
                    sp.dma_start(w_raw[:, c, 0, :], w_1[bass.ds(e, 1), :, cols].rearrange("a k n -> (a k) n")).then_inc(raw_ok[c], 16)
                    sp.dma_start(w_raw[:, c, 1, :], w_3[bass.ds(e, 1), :, cols].rearrange("a k n -> (a k) n")).then_inc(raw_ok[c], 16)
                    sp.dma_start(w_raw[:, c, 2, :], w_2[bass.ds(e, 1), cols, :].rearrange("a k n -> (a k) n")).then_inc(raw_ok[c], 16)

            load_expert(0)
            load_expert(1)
            for b in range(B):
                if b == 1:
                    load_expert(2, range(0, 2))
                half = slice(b * BANK, (b + 1) * BANK)
                sp.wait_ge(st_free, slot[("combT", b)] + 1)
                sp.dma_start(comb_dram[:, half], combT[:, half]).then_inc(comb_st, 16)
                sp.wait_ge(comb_st, 16 * (b + 1))
                for e in range(E):
                    sp.dma_start(cb[:, e, half], comb_dram[e:e + 1, half].partition_broadcast(P)).then_inc(cb_ok if e else cb_first[b], 16)
            load_expert(2, range(2, FC))
            with sp.Fori(3, E) as e:
                load_expert(e)
            out_v = out.rearrange("b (t p) d -> p (b t) d", p=P)
            for n, tiles in enumerate(OUT_PARTS):
                sp.wait_ge(o_ok, n + 1)
                sp.dma_start(out_v[:, tiles, :], xn[:, tiles, :]).then_inc(stored, 16)
            sp.wait_ge(stored, 16 * len(OUT_PARTS))

        @block.gpsimd
        def _(pool):
            pool.memset(ident[:, :], 0.0).then_inc(ident_z, 1)
            pool.wait_ge(ident_z, 1)
            pool.affine_select(out=ident[:, :], in_=ident[:, :], compare_op=ALU.not_equal, fill=1.0,
                               base=0, pattern=[[-1, P]], channel_multiplier=1).then_inc(ident_ok, 1)
            pool.memset(neg_half[:, :], HALF_ROOT).then_inc(const_ok, 1)
            pool.memset(lower[:, :, :], 1.0).then_inc(const_ok, 1)
            pool.wait_ge(const_ok, 2)
            pool.affine_select(out=lower[:, :, :], in_=lower[:, :, :], compare_op=ALU.is_gt, fill=0.0,
                               base=0, pattern=[[1, E], [-1, E]], channel_multiplier=0).then_inc(const_ok, 1)
            pool.memset(euler[:, :, :], E_BASE).then_inc(const_ok, 1)
            pool.memset(acc[:, :, :], 0.0).then_inc(acc_z, 1)

            def rstd_step(n):
                tiles = slice(norms[n].start, norms[n].stop)
                pool.wait_ge(ln_mv, normed_by[n])
                pool.tensor_scalar(rstd[:, tiles], mv[:, tiles, 1], EPS, None, ALU.add).then_inc(ln_pool, 1)
                pool.wait_ge(ln_pool, 2 * n + 1)
                pool.tensor_tensor(rstd[:, tiles], rstd[:, tiles], neg_half[:, tiles], ALU.pow).then_inc(ln_pool, 1)

            for n in range(4):
                rstd_step(n)

            def lo_part(e, c):
                pool.wait_ge(hi_w, split_count(e, c))
                pool.tensor_tensor(split_in(w_lo, xn_lo, e, c), w_raw[:, c, :, :], split_in(w_hi, xn_hi, e, c).bitcast(F32),
                                   ALU.subtract).then_inc(w_split, 1)

            def add_x(t):
                pool.wait_ge(st_free, slot[("y", t)] + 1)
                pool.tensor_tensor(x2[:, t, :], x_sb[:, t, :], xf[:, t, :], ALU.add).then_inc(x2_ok, 1)

            for t in range(T):
                if t >= LAG_T:
                    add_x(t - LAG_T)
                if t == T - 1:
                    lo_part(0, FIRST_SPLIT[0])
                if t - LAG_T == TB - 1:
                    rstd_step(4)
                pool.wait_ge(s_rcp, t + 1)
                pool.tensor_tensor(prob[:, t % NP_, :].rearrange("p (h m) -> p h m", h=H),
                                   prob[:, t % NP_, :].rearrange("p (h m) -> p h m", h=H),
                                   rowsum[:, t, :].rearrange("p (h o) -> p h o", o=1).broadcast_to([P, H, M]),
                                   ALU.mult).then_inc(s_norm, 1)
                if t == 0:
                    second = slice(TB, T)
                    pool.wait_ge(st_free, slot[("xnT", 2)] + 1)
                    pool.tensor_scalar(xn_hi[:, second, :], xnT[:, second, :], 1.0, 1.0, ALU.mult, ALU.mult).then_inc(xn_split, 1)
                    pool.wait_ge(xn_split, 1)
                    pool.tensor_tensor(xn_lo[:, second, :], xnT[:, second, :], xn_hi[:, second, :].bitcast(F32),
                                       ALU.subtract).then_inc(xn_ok[2], 1)
            lo_part(0, FIRST_SPLIT[1])
            lo_part(0, FIRST_SPLIT[2])
            for t in range(T - LAG_T, T - 1):
                add_x(t)
            rstd_step(5)
            lo_part(0, FIRST_SPLIT[3])
            add_x(T - 1)
            rstd_step(6)
            lo_part(1, 0)
            pool.wait_ge(r_pr, 2)
            pool.tensor_tensor(expo[1][:, :, :], euler[:, :, :], expo[1][:, :, :], ALU.pow).then_inc(r_exp1, 1)

            pool.wait_ge(acc_z, 1)
            pool.sem_inc(acc_ok, 2)

            def accumulate(e, halves=range(B)):
                for b in halves:
                    pool.wait_ge(y_used, 2 * e + (b + 3))
                    pool.wait_ge(acc_ok, 2 * e + (b + 1))
                    pool.tensor_tensor(acc[:, b, :], acc[:, b, :], y_c[:, b, :], ALU.add).then_inc(acc_ok, 1)

            for c in range(1, FC // 2):
                lo_part(1, c)
            with pool.Fori(1, E - 1) as e:
                for c in range(FC // 2, FC):
                    lo_part(e, c)
                lo_part(e + 1, 0)
                accumulate(e - 1)
                lo_part(e + 1, 1)
            for c in range(FC // 2, FC):
                lo_part(E - 1, c)
            accumulate(E - 2)
            accumulate(E - 1, [0])

        @block.scalar
        def _(act):
            act.dma_start(ctx_sb[:, :, :], ctx_in.rearrange("b m d -> m b d")).then_inc(ld["ctx"], 16)
            act.dma_start(x_sb[:, TB:T, :], x.rearrange("b (t p) d -> p (b t) d", p=P)[:, TB:T, :]).then_inc(ld["x1"], 16)
            act.dma_start(wq_sb[:, :], w_q[:, :]).then_inc(ld["wq"], 16)

            def empty_xnT(n, bank):
                tiles = slice(xn_tiles[n].start, xn_tiles[n].stop)
                for dst in (xn_hi, xnT) if n < 2 else (xnT,):
                    ins = act.activation(dst[:, tiles, :], bank[:, 0:len(xn_tiles[n]) * P].rearrange("p (a d) -> p a d", d=P),
                                         ACT.Identity, scale=gamma_sb, bias=beta_sb)
                return ins

            for n, (kind, i) in enumerate(plan):
                bank = psum[:, n % PB, :]
                act.wait_ge(pre_mm, n + 1)
                if kind == "ctxT":
                    ins = act.activation(ctxT[:, :], bank[:, 0:B * M], ACT.Copy)
                elif kind == "vecs":
                    ins = act.activation(vecs[:, :], bank[:, 0:VECS], ACT.Copy)
                elif kind == "wqT":
                    ins = act.activation(wqT[:, 4 * i:4 * i + 4, :], bank.rearrange("p (a d) -> p a d", d=P), ACT.Copy)
                elif kind == "kT":
                    g = kv_groups[i]
                    ins = act.activation(kT[:, g.start:g.stop, :],
                                         bank[:, 0:len(g) * B * M].rearrange("p (a m) -> p a m", a=len(g)), ACT.Copy)
                elif kind == "xnT":
                    if i == 0:
                        act.wait_ge(pre_act, place[("vecs", 0)] + 1)
                    ins = empty_xnT(i, bank)
                else:
                    par, g = h_groups[i]
                    ins = act.activation(head_cols(g_hi, par, g), bank_heads(bank, g), ACT.Copy, scale=SCALE)
                ins.then_inc(pre_act, 1)

            def logits_of(b):
                return stage_bank(("logits", b))[:, 0:TB * E].rearrange("p (t e) -> p t e", e=E)

            def w_hi_part(e, c):
                act.wait_ge(raw_ok[c], 48 * e + 48)
                if isinstance(e, int) and e == 0:
                    if c < 2:
                        act.wait_ge(s_mm, T)
                elif not isinstance(e, int) or e > 1 or c >= 2:
                    act.wait_ge(g2_ok, HB + 2 * FC * e + (2 * c + 2 - 2 * FC))
                act.activation(split_in(w_hi, xn_hi, e, c), w_raw[:, c, :, :], ACT.Copy).then_inc(hi_w, 1)

            def empty_stage(key, dst, src):
                act.wait_ge(st_mm, slot[key] + 1)
                act.activation(dst, src, ACT.Copy).then_inc(st_free, 1)

            def empty_xfT(b):
                half = slice(b * BANK, (b + 1) * BANK)
                act.wait_ge(st_mm, slot[("xfT", b)] + 1)
                act.activation(xf_hi[:, half], stage_bank(("xfT", b)), ACT.Copy).then_inc(xf_hi_ok, 1)
                act.activation(xfT[:, half], stage_bank(("xfT", b)), ACT.Copy).then_inc(st_free, 1)

            def exps(t):
                act.wait_ge(s_sub, t + 1)
                act.activation(prob[:, t % NP_, :], prob[:, t % NP_, :], ACT.Exp).then_inc(s_exp, 1)

            for i, g in enumerate(kv_groups):
                empty_stage(("vT", i), vT[:, g.start:g.stop, :],
                            stage_bank(("vT", i))[:, 0:len(g) * B * M].rearrange("p (a m) -> p a m", a=len(g)))
            exps(0)
            for i, (par, g) in enumerate(h_groups):
                act.wait_ge(st_mm, slot[("voT", i)] + 1)
                act.activation(head_cols(voT, par, g), bank_heads(stage_bank(("voT", i)), g), ACT.Copy).then_inc(st_free, 1)
                if i == 1:
                    exps(1)

            def empty_chunks(key, g, dst):
                full = [c for c in g if rows(c) == P]
                src = stage_bank(key).rearrange("p (a d) -> p a d", d=P)
                ins = act.activation(dst[:, full[0]:full[-1] + 1, :], src[:, 0:len(full), :], ACT.Copy)
                if len(full) < len(g):
                    c = g[-1]
                    ins = act.activation(dst[0:rows(c), c, :], src[0:rows(c), len(full), :], ACT.Copy)
                ins.then_inc(st_free, 1)

            act.wait_ge(st_mm, slot[("xnT", 2)] + 1)
            empty_xnT(2, stage_bank(("xnT", 2))).then_inc(st_free, 1)
            for i, (b, g) in enumerate(vo_groups):
                act.wait_ge(st_mm, slot[("vo", i)] + 1)
                empty_chunks(("vo", i), g, vo[:, b])
                if i == EARLY_VO - 1:
                    exps(2)
            for t in range(T):
                for i, g in enumerate(pt_groups):
                    act.wait_ge(st_mm, slot[("pT", t, i)] + 1)
                    if i == 0 and t >= 2:
                        act.wait_ge(st_mm, slot[("y", t - 2)] + 1)
                    empty_chunks(("pT", t, i), g, probT[:, t % 2])
                if t + LAG_T < T:
                    exps(t + LAG_T)
                if t == T - 2:
                    empty_stage(("logits", 0), lg[:, :, :], logits_of(0))
                    act.wait_ge(r_pr, 1)
                    act.activation(pr[:, :, :], pr[:, :, :], ACT.Exp).then_inc(r_act, 1)
                    act.wait_ge(r_act, 1)
                    act.preload_act_table(ACT.Silu)
                if t in SPLIT_AT:
                    w_hi_part(0, FIRST_SPLIT[SPLIT_AT.index(t)])
                if t < T - 1:
                    empty_stage(("y", t), xf[:, t, :], stage_bank(("y", t))[:, 0:P])
                if t == T - 3:
                    empty_xfT(0)

            def experts(e, first, last):
                if not first:
                    hi_part(2 * FC * e - 1, (2 * FC - 1) % HB)
                act.activation(b1_now[:, :], b13T[:, 0, bass.ds(FC * e, FC)], ACT.Copy).then_inc(b1_ok, 1)
                for j, (c, _) in enumerate(order_of(e)):
                    u = 2 * FC * e + j
                    act.wait_ge(g1a, u + 1)
                    act.wait_ge(gate_ok, u + 1)
                    if j == 0:
                        act.wait_ge(b1_ok, e + 1)
                    act.activation(silu[:, j % 2, :], psum[:, j % 2, :], ACT.Silu,
                                   bias=b1_now[:, c:c + 1]).then_inc(silu_ok, 1)
                    if first and j == 0:
                        empty_stage(("y", T - 1), xf[:, T - 1, :], stage_bank(("y", T - 1))[:, 0:P])
                    if first and j == 2:
                        empty_xfT(1)
                    if j > 0:
                        hi_part(u - 1, (j - 1) % HB)
                    if isinstance(e, int) and e == 1 and j == 2:
                        empty_combT(1)
                    if first and j == 3:
                        empty_stage(("logits", 1), logit[1][:, :, :], logits_of(1))
                    elif first and j == 6:
                        empty_combT(0)
                    if first and j in (3, 5):
                        w_hi_part(1, j // 2 - 1)
                    elif j in (1, 3) and not first:
                        w_hi_part(e, FC // 2 + j // 2)
                    elif j in (5, 7) and not first and not last:
                        w_hi_part(e + 1, j // 2 - FC // 2)

            def empty_combT(b):
                empty_stage(("combT", b), combT[:, b * BANK:(b + 1) * BANK], stage_bank(("combT", b))[0:E, :])

            def hi_part(u, slot_h):
                act.wait_ge(gate_ok, u + 3)
                act.wait_ge(g2_ok, u + 1)
                act.activation(h_hi[:, slot_h, :], h[:, slot_h % 2, :], ACT.Copy).then_inc(hhi_ok, 1)

            experts(0, True, False)
            experts(1, False, False)
            with act.Fori(2, E - 1) as e:
                experts(e, False, False)
            experts(E - 1, False, True)
            hi_part(2 * FC * E - 1, (2 * FC - 1) % HB)

        @block.vector
        def _(dve):
            def copy_bank(n, kind, i):
                bank = psum[:, n % PB, :]
                dve.wait_ge(pre_mm, n + 1)
                par, g = h_groups[i]
                dve.wait_ge(pre_act, empties(n, "a"))
                dve.scalar_tensor_tensor(
                    out=head_cols(g_lo, par, g), in0=bank_heads(bank, g), scalar=SCALE,
                    in1=head_cols(g_hi, par, g).bitcast(F32), op0=ALU.mult, op1=ALU.subtract).then_inc(pre_dve, 1)

            stat = [0]

            def ln_stats(src, tiles):
                for t in tiles:
                    dve.bn_stats(stats[:, t, :], src[:, t, :]).then_inc(ln_stat, 1)
                    stat[0] += 1
                for k, t in enumerate(tiles):
                    dve.wait_ge(ln_stat, stat[0] - len(tiles) + k + 1)
                    dve.bn_aggr(mv[:, t, :], stats[:, t, :]).then_inc(ln_mv, 1)

            def ln_apply(n, src, dst):
                dve.wait_ge(ln_pool, 2 * n + 2)
                for t in norms[n]:
                    dve.tensor_scalar(dst[:, t, :], src[:, t, :], mv[:, t, 0:1], rstd[:, t:t + 1],
                                      ALU.subtract, ALU.mult).then_inc(ln_out, 1)

            dve.wait_ge(ld["x0"], 16)
            ln_stats(x_sb, halves[0])
            ln_apply(0, x_sb, xn)
            dve.wait_ge(ln_out, TB)
            ln_stats(xn, halves[0])
            dve.wait_ge(ld["x1"], 16)
            ln_stats(x_sb, halves[1])
            ln_apply(1, xn, xn)
            ln_apply(2, x_sb, xn)
            for n, (kind, i) in enumerate(plan):
                if kind == "g":
                    copy_bank(n, kind, i)
                elif kind == "xnT":
                    if i == 1:
                        dve.wait_ge(ln_out, 3 * TB)
                        ln_stats(xn, halves[1])
                    tiles = slice(xn_tiles[i].start, xn_tiles[i].stop)
                    dve.wait_ge(pre_act, empties(n, "a"))
                    dve.tensor_tensor(xn_lo[:, tiles, :], xnT[:, tiles, :], xn_hi[:, tiles, :].bitcast(F32),
                                      ALU.subtract).then_inc(xn_ok[i], 1)

            def scores(t):
                return psum[:, 3 * (t % 2):3 * (t % 2) + 3, :].rearrange("p a n -> p (a n)")[:, 0:HM].rearrange("p (h m) -> p h m", h=H)

            def heads(t):
                return prob[:, t % NP_, :].rearrange("p (h m) -> p h m", h=H)

            chain = [0]

            def sums(t):
                dve.wait_ge(s_exp, t + 1)
                dve.tensor_reduce(rowsum[:, t, :], heads(t), AX.X, ALU.add).then_inc(s_dve, 1)
                chain[0] += 1
                dve.wait_ge(s_dve, chain[0])
                dve.reciprocal(rowsum[:, t, :], rowsum[:, t, :]).then_inc(s_rcp, 1)

            for t in range(T):
                dve.wait_ge(s_mm, t + 1)
                dve.tensor_reduce(negmax[:, t, :], scores(t), AX.X, ALU.max, negate=True).then_inc(s_dve, 1)
                chain[0] += 1
                dve.wait_ge(s_dve, chain[0])
                if t >= NP_:
                    dve.wait_ge(st_mm, slot[("pT", t - NP_, len(pt_groups) - 1)] + 1)
                dve.tensor_tensor(heads(t), scores(t),
                                  negmax[:, t, :].rearrange("p (h o) -> p h o", o=1).broadcast_to([P, H, M]),
                                  ALU.add).then_inc(s_sub, 1)
                if t == 0:
                    ln_apply(3, xn, xn)
                for k in {T - 3: [0], T - 2: [1], T - 1: [2, 3]}.get(t, []):
                    dve.wait_ge(x2_ok, k + 1)
                    ln_stats(x2, [k])
                if t >= 1:
                    sums(t - 1)
            ln_apply(4, x2, xf)
            sums(T - 1)
            dve.wait_ge(s_sub, T)
            dve.sem_inc(gate_ok, 2)
            dve.sem_inc(y_used, 2)
            dve.wait_ge(ld["router"], 32)
            dve.wait_ge(const_ok, 4)
            route = [0]

            def link(ins):
                ins.then_inc(r_dve, 1)
                route[0] += 1
                dve.wait_ge(r_dve, route[0])

            def over_e(a):
                return a.rearrange("p (t o) -> p t o", o=1).broadcast_to([P, TB, E])

            def xf_lo_part(b):
                half = slice(b * BANK, (b + 1) * BANK)
                dve.wait_ge(xf_hi_ok, b + 1)
                dve.wait_ge(st_free, slot[("xfT", b)] + 1)
                dve.tensor_tensor(xf_lo[:, half], xfT[:, half], xf_hi[:, half].bitcast(F32), ALU.subtract).then_inc(xf_lo_ok, 1)

            def shift_logits(b):
                lgb = logit[b]
                dve.wait_ge(st_free, slot[("logits", b)] + 1)
                link(dve.tensor_tensor(lgb[:, :, :], lgb[:, :, :],
                                       bg_sb[:, :].rearrange("p (o e) -> p o e", o=1).broadcast_to([P, TB, E]), ALU.add))
                link(dve.tensor_reduce(red[:, :], lgb[:, :, :], AX.X, ALU.max))
                dve.tensor_tensor(expo[b][:, :, :], lgb[:, :, :], over_e(red[:, :]), ALU.subtract).then_inc(r_pr, 1)

            def rank_logits(b):
                lgb = logit[b]
                other = lgb[:, :, :].rearrange("p t (o e) -> p t o e", o=1).broadcast_to([P, TB, E, E])
                me = lgb[:, :, :].rearrange("p t (e o) -> p t e o", o=1).broadcast_to([P, TB, E, E])
                for dst, op in ((cmp_a, ALU.is_gt), (cmp_b, ALU.is_equal)):
                    dve.tensor_tensor(dst[:, :, :].rearrange("p (t e) f -> p t e f", t=TB), other, me, op).then_inc(r_dve, 1)
                    route[0] += 1
                dve.wait_ge(r_dve, route[0])
                low4 = lower[:, :, :].rearrange("p e f -> p (e f)").rearrange("p (o n) -> p o n", o=1).broadcast_to([P, TB, E * E])
                b4 = cmp_b[:, :, :].rearrange("p (t e) f -> p t (e f)", t=TB)
                link(dve.tensor_tensor(b4, b4, low4, ALU.mult))
                link(dve.tensor_tensor(cmp_a[:, :, :], cmp_a[:, :, :], cmp_b[:, :, :], ALU.add))
                link(dve.tensor_reduce(rank[:, :, :].rearrange("p t e -> p (t e)"), cmp_a[:, :, :], AX.X, ALU.add))
                link(dve.tensor_scalar(rank[:, :, :], rank[:, :, :], 2.0, None, ALU.is_lt))

            def combine_weights(b):
                prb = expo[b]
                dve.wait_ge(r_exp1 if b else r_act, 1)
                link(dve.tensor_reduce(red[:, :], prb[:, :, :], AX.X, ALU.add))
                link(dve.reciprocal(red[:, :], red[:, :]))
                link(dve.tensor_tensor(prb[:, :, :], prb[:, :, :], over_e(red[:, :]), ALU.mult))
                link(dve.tensor_tensor(prb[:, :, :], prb[:, :, :], rank[:, :, :], ALU.mult))
                link(dve.tensor_reduce(red[:, :], prb[:, :, :], AX.X, ALU.add))
                link(dve.tensor_scalar(red[:, :], red[:, :], 1e-6, None, ALU.add))
                link(dve.reciprocal(red[:, :], red[:, :]))
                dve.tensor_tensor(comb[:, b * TB:(b + 1) * TB, :], prb[:, :, :], over_e(red[:, :]), ALU.mult).then_inc(comb_ok, 1)

            def late_stats(t):
                dve.wait_ge(x2_ok, t + 1)
                ln_stats(x2, [t])

            xf_lo_part(0)
            shift_logits(0)
            late_stats(T - 4)
            late_stats(T - 3)
            rank_logits(0)
            late_stats(T - 2)
            combine_weights(0)

            def lo_part(u, j):
                dve.wait_ge(hhi_ok, u + 1)
                dve.tensor_tensor(h_lo[:, j % HB, :], h[:, j % 2, :], h_hi[:, j % HB, :].bitcast(F32),
                                  ALU.subtract).then_inc(hlo_ok, 1)

            def combine(e, b, cols=slice(0, BANK)):
                dve.wait_ge(g2_ok, 2 * FC * e + (HB + 1 + max(j for j, (_, half) in enumerate(order_of(e)) if half == b)))
                dve.wait_ge(acc_ok, 2 * e + (b + 1))
                dve.scalar_tensor_tensor(out=y_c[:, b, cols], in0=y_bank(e, b)[:, cols], scalar=b2T[:, bass.ds(e, 1)],
                                         in1=cb[:, bass.ds(e, 1), b * BANK + cols.start:b * BANK + cols.stop]
                                         .rearrange("p a n -> p (a n)"),
                                         op0=ALU.add, op1=ALU.mult).then_inc(y_used, 1)

            def gate(e, j, c):
                u = 2 * FC * e + j
                if not isinstance(u, int) or u >= 2:
                    dve.wait_ge(hlo_ok, u - 1)
                dve.wait_ge(g1b, u + 1)
                dve.wait_ge(silu_ok, u + 1)
                dve.scalar_tensor_tensor(out=h[:, j % 2, :], in0=psum[:, 2 + j % 2, :],
                                         scalar=b13T[:, 1, bass.ds(FC * e + c, 1)], in1=silu[:, j % 2, :],
                                         op0=ALU.add, op1=ALU.mult).then_inc(gate_ok, 1)

            def finish_norm():
                ln_apply(5, x2, xf)
                late_stats(T - 1)
                ln_apply(6, x2, xf)

            def experts(e, first):
                between = {0: finish_norm, 2: lambda: xf_lo_part(1), 3: lambda: shift_logits(1),
                           4: lambda: rank_logits(1), 7: lambda: combine_weights(1)} if first else {}
                for j, (c, _) in enumerate(order_of(e)):
                    gate(e, j, c)
                    if j > 0 or not first:
                        lo_part(2 * FC * e + j - 1, (j - 1) % HB)
                    if j in between:
                        between[j]()
                    if 0 < j <= B and not (isinstance(e, int) and e < 2):
                        combine(e - 1, j - 1)
                    if isinstance(e, int) and e == 1 and j in (5, 6):
                        dve.wait_ge(cb_first[j - 5], 16)
                        combine(0, j - 5)

            experts(0, True)
            experts(1, False)
            dve.wait_ge(cb_ok, 16 * (E - 1) * B)
            with dve.Fori(2, E - 1) as e:
                experts(e, False)
            experts(E - 1, False)
            lo_part(2 * FC * E - 1, (2 * FC - 1) % HB)
            combine(E - 1, 0)
            for n, tiles in enumerate(OUT_PARTS[1:]):
                cols = slice(tiles.start * P - BANK, tiles.stop * P - BANK)
                combine(E - 1, 1, cols)
                dve.wait_ge(y_used, 2 * E + 2 + n)
                dve.tensor_tensor(acc[:, 1, cols], acc[:, 1, cols], y_c[:, 1, cols], ALU.add).then_inc(acc_last, 1)
            for n, tiles in enumerate(OUT_PARTS):
                dve.wait_ge(o_mm, n + 1)
                dve.tensor_tensor(xn[:, tiles, :], x2[:, tiles, :], out_bank(tiles), ALU.add).then_inc(o_ok, 1)

        @block.tensor
        def _(pe):
            def mm3(dst, w_h, w_l, m_h, m_l):
                pe.matmul(dst, w_h, m_h, start=True, stop=False)
                pe.matmul(dst, w_l, m_h, start=False, stop=False)
                return pe.matmul(dst, w_h, m_l, start=False, stop=True)

            def open_pre(n):
                if n >= PB:
                    for who, s in (("a", pre_act), ("d", pre_dve)):
                        if who in emptied_by[plan[n - PB][0]]:
                            pe.wait_ge(s, empties(n - PB, who))
                return psum[:, n % PB, :]

            def both_parities(banks, g, done, left, right):
                for k, pair in enumerate(g):
                    for par in range(2):
                        r = slice(DH * par, DH * par + DH)
                        ins = pe.matmul(bank_heads(banks[par], g)[:, :, k * M:(k + 1) * M], left[r, pair, :],
                                        right[r, pair, :].rearrange("p (b m) -> p b m", b=B),
                                        start=True, stop=True)
                        if k == len(g) - 1:
                            ins.then_inc(done, 1)

            def tokens_T(n, bank):
                pe.wait_ge(ln_out, 2 * TB * (n // 2 + 1))
                for k, t in enumerate(xn_tiles[n]):
                    ins = pe.transpose(bank[:, k * P:(k + 1) * P], xn[:, t, :], ident[:, :])
                return ins

            pe.wait_ge(ident_ok, 1)
            def warm_up(n):
                for k in range(n):
                    pe.transpose(psum[:, PB - 1, 0:P], ident[:, :], ident[:, :])

            warm_up(10)
            for n, (kind, i) in enumerate(plan):
                if kind == "g":
                    par, g = h_groups[i]
                    pe.wait_ge(pre_act, empties(place[("wqT", (g.stop - 1) // 4)], "a"))
                    if par == 0:
                        both_parities([open_pre(n), open_pre(n + 1)], g, pre_mm, wqT, kT)
                    continue
                bank = open_pre(n)
                if kind == "ctxT":
                    pe.wait_ge(ld["ctx"], 16)
                    for b in range(B):
                        ins = pe.transpose(bank[:, b * M:(b + 1) * M], ctx_sb[:, b, :], ident[0:M, 0:M])
                    ins.then_inc(pre_mm, 1)
                    warm_up(5)
                    continue
                elif kind == "vecs":
                    pe.wait_ge(ld["vecs"], 80)
                    ins = pe.transpose(bank[:, 0:VECS], vec_rows[:, :], ident[0:VECS, 0:VECS])
                elif kind == "wqT":
                    if i == 0:
                        pe.wait_ge(ld["wq"], 16)
                    for k in range(4):
                        pair = 4 * i + k
                        ins = pe.transpose(bank[:, k * P:(k + 1) * P], wq_sb[:, pair * P:(pair + 1) * P], ident[:, :])
                elif kind == "xnT":
                    ins = tokens_T(i, bank)
                else:
                    if i == 0:
                        pe.wait_ge(ld["wk"], 16)
                        pe.wait_ge(pre_act, 1)
                    for k, pair in enumerate(kv_groups[i]):
                        ins = pe.matmul(bank[:, k * B * M:(k + 1) * B * M], wkv_sb[:, pair * P:(pair + 1) * P],
                                        ctxT[:, :], start=True, stop=True)
                ins.then_inc(pre_mm, 1)

            def score_mm(t):
                b = t // TB
                for n, tiles in enumerate(xn_tiles):
                    if t == tiles.start:
                        pe.wait_ge(xn_ok[n], 1)
                if t >= 2:
                    pe.wait_ge(s_sub, t - 1)
                for k in range(3):
                    cols = slice(k * BANK, min((k + 1) * BANK, HM))
                    ins = mm3(psum[:, 3 * (t % 2) + k, 0:cols.stop - cols.start], xn_hi[:, t, :], xn_lo[:, t, :],
                              g_hi[:, b, cols], g_lo[:, b, cols])
                ins.then_inc(s_mm, 1)

            def open_stage(key):
                if before[key] and not (key in OWN and before[key][0] == "voT"):
                    pe.wait_ge(st_free, slot[before[key]] + 1)
                elif key in OWN:
                    pe.wait_ge(s_sub, 2 if key[0] == "voT" else T if OWN[key] >= 3 else T - 1)
                return stage_bank(key)

            def value_T(i):
                bank = open_stage(("vT", i))
                for k, pair in enumerate(kv_groups[i]):
                    ins = pe.matmul(bank[:, k * B * M:(k + 1) * B * M],
                                    wkv_sb[:, INNER + pair * P:INNER + (pair + 1) * P], ctxT[:, :], start=True, stop=True)
                ins.then_inc(st_mm, 1)

            def value_out(i):
                pe.wait_ge(st_free, slot[("vT", i // 2)] + 1)
                both_parities([open_stage(("voT", i)), open_stage(("voT", i + 1))], h_groups[i][1], st_mm, wout_sb, vT)

            def emptied(n):
                pe.wait_ge(pre_act, empties(n, "a"))
                pe.wait_ge(pre_dve, empties(n, "d"))

            pe.wait_ge(ld["wv"], 16)
            emptied(max(n for n in range(len(plan)) if n % PB == 7))
            value_T(0)
            emptied(place[("g", len(h_groups) - 1)])
            score_mm(0)
            emptied(len(plan) - 1)
            for i in range(1, len(kv_groups)):
                value_T(i)
            score_mm(1)
            pe.wait_ge(ld["wout"], 16)
            value_out(0)
            score_mm(2)
            for i in range(2, len(h_groups), 2):
                value_out(i)
            tokens_T(2, open_stage(("xnT", 2))).then_inc(st_mm, 1)

            def value_chunks(i):
                b, g = vo_groups[i]
                pe.wait_ge(st_free, slot[("voT", len(h_groups) - 1)] + 1)
                bank = open_stage(("vo", i))
                for k, c in enumerate(g):
                    ins = pe.transpose(bank[0:rows(c), k * P:(k + 1) * P], voT[:, b, c * P:c * P + rows(c)], ident[:, :])
                ins.then_inc(st_mm, 1)

            def router_mm(kind, b):
                bank = open_stage((kind, b))
                if kind == "xfT":
                    pe.wait_ge(ln_out, 2 * T + TB * (b + 1))
                elif kind == "logits":
                    pe.wait_ge(st_free, slot[("xfT", b)] + 1)
                else:
                    pe.wait_ge(comb_ok, b + 1)
                for k in range(TB):
                    t = TB * b + k
                    if kind == "xfT":
                        ins = pe.transpose(bank[:, k * P:(k + 1) * P], xf[:, t, :], ident[:, :])
                    elif kind == "logits":
                        ins = pe.matmul(bank[:, k * E:(k + 1) * E], xfT[:, t * P:(t + 1) * P], wg_sb[:, :],
                                        start=True, stop=True)
                    else:
                        ins = pe.transpose(bank[0:E, k * P:(k + 1) * P], comb[:, t, :], ident[:, :])
                ins.then_inc(st_mm, 1)

            pe.wait_ge(ld["router"], 32)
            LAG = 3

            def up(e, j):
                c, b = order_of(e)[j]
                w_h, w_l = split_in(w_hi, xn_hi, e, c), split_in(w_lo, xn_lo, e, c)
                u = 2 * FC * e + j
                half = slice(b * BANK, (b + 1) * BANK)
                pe.wait_ge(w_split, split_count(e, c))
                pe.wait_ge(gate_ok, u + 1)
                mm3(psum[:, j % 2, :], w_h[:, 0, :], w_l[:, 0, :], xf_hi[:, half], xf_lo[:, half]).then_inc(g1a, 1)
                mm3(psum[:, 2 + j % 2, :], w_h[:, 1, :], w_l[:, 1, :], xf_hi[:, half], xf_lo[:, half]).then_inc(g1b, 1)

            def down(e, j):
                order = order_of(e)
                c, b = order[j]
                w_h, w_l = split_in(w_hi, xn_hi, e, c), split_in(w_lo, xn_lo, e, c)
                mine = [k for k, (_, half) in enumerate(order) if half == b]
                u = 2 * FC * e + j
                pe.wait_ge(hlo_ok, u + 1)
                if j == mine[0] and isinstance(e, int) and e < 2:
                    pe.wait_ge(st_free, slot[("combT", B - 1) if e else ("y", T - 1)] + 1)
                elif j == mine[0]:
                    pe.wait_ge(y_used, 2 * e + (b + 1))
                dst = y_bank(e, b)
                pe.matmul(dst, w_h[:, 2, :], h_hi[:, j % HB, :], start=(j == mine[0]), stop=False)
                pe.matmul(dst, w_l[:, 2, :], h_hi[:, j % HB, :], start=False, stop=False)
                pe.matmul(dst, w_h[:, 2, :], h_lo[:, j % HB, :], start=False, stop=(j == mine[-1])).then_inc(g2_ok, 1)

            def steady(e):
                for j in range(2 * FC):
                    k = j + LAG
                    up(e + k // (2 * FC), k % (2 * FC)) if k >= 2 * FC else up(e, k)
                    down(e, j)

            for i in range(len(vo_groups)):
                value_chunks(i)
                if i == EARLY_VO - 1:
                    for t in range(3, LEAD):
                        score_mm(t)
            pe.wait_ge(ld["router"], 32)
            for t in range(T):
                pe.wait_ge(s_norm, t + 1)
                for i, g in enumerate(pt_groups):
                    if i == len(pt_groups) - 1:
                        if t + LEAD < T:
                            score_mm(t + LEAD)
                        elif t == T - 1:
                            pe.wait_ge(xf_lo_ok, 1)
                            pe.wait_ge(st_free, slot[("y", T - 2)] + 1)
                            up(0, 0)
                    bank = open_stage(("pT", t, i))
                    for k, c in enumerate(g):
                        ins = pe.transpose(bank[0:rows(c), k * P:(k + 1) * P], prob[:, t % NP_, c * P:c * P + rows(c)], ident[:, :])
                    ins.then_inc(st_mm, 1)
                if t == T - 2:
                    router_mm("logits", 0)
                bank = open_stage(("y", t))
                if t == 0:
                    pe.wait_ge(st_free, slot[("vo", len(vo_groups) - 1)] + 1)
                for c in range(CH):
                    if c % 4 == 0:
                        pe.wait_ge(st_free, slot[("pT", t, c // 4)] + 1)
                    ins = pe.matmul(bank[:, 0:P], probT[0:rows(c), t % 2, c, :], vo[0:rows(c), t // TB, c, :],
                                    start=(c == 0), stop=(c == CH - 1))
                ins.then_inc(st_mm, 1)
                if t == T - 3:
                    router_mm("xfT", 0)

            pe.sem_inc(g2_ok, HB)
            up(0, 1)
            up(0, 2)
            router_mm("xfT", 1)
            for j in range(2 * FC):
                k = j + LAG
                if k == FC:
                    pe.wait_ge(xf_lo_ok, 2)
                up(1, k - 2 * FC) if k >= 2 * FC else up(0, k)
                down(0, j)
                if j == 0:
                    router_mm("logits", 1)
                elif j in (3, 7):
                    router_mm("combT", j // 4)
            steady(1)
            with pe.Fori(2, E - 1) as e:
                steady(e)
            for j in range(2 * FC):
                if j + LAG < 2 * FC:
                    up(E - 1, j + LAG)
                down(E - 1, j)
            for n, tiles in enumerate(OUT_PARTS):
                pe.wait_ge(*((acc_last, n) if n else (acc_ok, 2 * E + 1)))
                for k, t in enumerate(range(tiles.start, tiles.stop)):
                    ins = pe.transpose(out_bank(tiles)[:, k, :], acc[:, t // TB, (t % TB) * P:(t % TB + 1) * P], ident[:, :])
                ins.then_inc(o_mm, 1)


_INS = ['x', 'ctx_1024', 'L0_xattn_W_q', 'L0_xattn_W_kv', 'L0_xattn_W_out', 'L0_xattn_ln_gamma', 'L0_xattn_ln_beta',
        'L0_ffn_Wg', 'L0_ffn_bg', 'L0_ffn_W1', 'L0_ffn_b1', 'L0_ffn_W3', 'L0_ffn_b3', 'L0_ffn_W2', 'L0_ffn_b2']
_OUTS = [((2, 512, 128), 'float32')]


def kernel(**inputs):
    import numpy as _np
    import concourse.bacc as _bacc
    from concourse import mybir as _mybir
    from concourse.bass_utils import run_bass_kernel_spmd as _run

    nc = _bacc.Bacc("TRN2", target_bir_lowering=False, num_devices=1)
    arrays, args = {}, []
    for name in _INS:
        a = _np.ascontiguousarray(inputs[name])
        arrays[f"in_{name}_dram"] = a
        args.append(nc.dram_tensor(f"in_{name}_dram", a.shape, _mybir.dt.from_np(a.dtype), kind="ExternalInput").ap())
    for i, (shape, dtype) in enumerate(_OUTS):
        dt = _mybir.dt.from_np(_np.dtype(dtype))
        args.append(nc.dram_tensor(f"out_{i}_dram", shape, dt, kind="ExternalOutput").ap())
    build(nc, *args)
    r = _run(nc, [arrays], core_ids=[0])
    got = tuple(r.results[0][f"out_{i}_dram"] for i in range(len(_OUTS)))
    return got[0]
```
